# Optimizing a Trainium2 kernel written in Bass

```python
import numpy as np
import jax
import jax.numpy as jnp

def _softmax(x, axis=-1):
    return jax.nn.softmax(x, axis=axis)

def _gelu(x):
    return jax.nn.gelu(x, approximate=True)

def _silu(x):
    return jax.nn.silu(x)

def _sigmoid(x):
    return jax.nn.sigmoid(x)

def _layernorm(x, axis=-1, eps=1e-05):
    m = jnp.mean(x, axis=axis, keepdims=True)
    v = jnp.var(x, axis=axis, keepdims=True)
    return (x - m) / jnp.sqrt(v + eps)

def _scatter_add(tgt, idx, src, axis=0):
    return tgt.at[idx].add(src)

def _segment_sum(src, seg, n):
    return jax.ops.segment_sum(src, seg, n)
kernel_name = 'mk_prb_d1_jaxref_r4_bec8d0'

def setup_inputs(seed: int=0):
    np.random.seed(seed)
    _w = jnp.asarray

    def _L0_attn_setup():
        import jax, jax.numpy as jnp
        from jax import lax
        import numpy as np
        DIM = 256
        H = 8
        DK = 128
        DV = 64
        GATE_NORM = 16.0

        def _gla(x, Wq, Wk, Wv, Wo, Wg, bg, Wog):
            B, S, D = x.shape
            q = (x @ Wq).reshape(B, S, H, DK)
            k = (x @ Wk).reshape(B, S, H, DK) * DK ** (-0.5)
            v = (x @ Wv).reshape(B, S, H, DV)
            alpha = jax.nn.sigmoid((x @ Wg + bg) / GATE_NORM)

            def step(state, inp):
                qt, kt, vt, at = inp
                state = at[..., None, None] * state + kt[..., None] * vt[:, :, None, :]
                out_t = jnp.einsum('bhk,bhkv->bhv', qt, state)
                return (state, out_t)
            state0 = jnp.zeros((B, H, DK, DV), x.dtype)
            xs = (jnp.moveaxis(q, 1, 0), jnp.moveaxis(k, 1, 0), jnp.moveaxis(v, 1, 0), jnp.moveaxis(alpha, 1, 0))
            _, outs = lax.scan(step, state0, xs)
            out = jnp.moveaxis(outs, 0, 1).reshape(B, S, H * DV)
            og = jax.nn.sigmoid(x @ Wog)
            return out * og @ Wo
        key = jax.random.key(seed)
        ks = jax.random.split(key, 8)
        B, S = (2, 1024)

        def xavier(k, shape, gain=1.0):
            fan_in, fan_out = (shape[0], shape[1])
            lim = gain * np.sqrt(6.0 / (fan_in + fan_out))
            return jax.random.uniform(k, shape, jnp.float32, -lim, lim)
        g = 2 ** (-2.5)
        return {'x': jax.random.normal(ks[0], (B, S, DIM), jnp.float32), 'Wq': xavier(ks[1], (DIM, H * DK), g), 'Wk': xavier(ks[2], (DIM, H * DK), g), 'Wv': xavier(ks[3], (DIM, H * DV), g), 'Wo': xavier(ks[4], (H * DV, DIM)), 'Wg': xavier(ks[5], (DIM, H)), 'bg': jnp.zeros((H,), jnp.float32), 'Wog': xavier(ks[6], (DIM, H * DV))}
    _L0_attn_in = _L0_attn_setup()

    def _L0_ffn_setup():
        import jax, jax.numpy as jnp
        import numpy as np
        B, S, H, I = (2, 512, 256, 128)
        E, K, G, TG = (64, 8, 8, 4)
        SCALE = 2.5
        CAP = 256
        key = jax.random.key(seed)
        ks = jax.random.split(key, 6)
        hidden_states = jax.random.normal(ks[0], (B, S, H), jnp.float32)
        gate_w = jax.random.normal(ks[1], (E, H), jnp.float32) * 0.02
        gate_bias = jax.random.normal(ks[2], (E,), jnp.float32) * 0.02
        w_gate = jax.random.normal(ks[3], (E, H, I), jnp.float32) * (1.0 / np.sqrt(H))
        w_up = jax.random.normal(ks[4], (E, H, I), jnp.float32) * (1.0 / np.sqrt(H))
        w_down = jax.random.normal(ks[5], (E, I, H), jnp.float32) * (1.0 / np.sqrt(I))
        return {'hidden_states': hidden_states, 'gate_w': gate_w, 'gate_bias': gate_bias, 'w_gate': w_gate, 'w_up': w_up, 'w_down': w_down}
    _L0_ffn_in = _L0_ffn_setup()
    _d = {'L0_attn_x': _L0_attn_in['x'], 'L0_attn_Wq': _L0_attn_in['Wq'], 'L0_attn_Wk': _L0_attn_in['Wk'], 'L0_attn_Wv': _L0_attn_in['Wv'], 'L0_attn_Wo': _L0_attn_in['Wo'], 'L0_attn_Wg': _L0_attn_in['Wg'], 'L0_attn_bg': _L0_attn_in['bg'], 'L0_attn_Wog': _L0_attn_in['Wog'], 'L0_ffn_gate_w': _L0_ffn_in['gate_w'], 'L0_ffn_gate_bias': _L0_ffn_in['gate_bias'], 'L0_ffn_w_gate': _L0_ffn_in['w_gate'], 'L0_ffn_w_up': _L0_ffn_in['w_up'], 'L0_ffn_w_down': _L0_ffn_in['w_down']}
    _x0 = _d['L0_attn_x']
    _d['L0_attn_x'] = jax.random.normal(jax.random.fold_in(jax.random.key(seed), 1), (4, 2048, 256), dtype=_x0.dtype)
    del _x0
    return _d

def reference(L0_attn_x, L0_attn_Wq, L0_attn_Wk, L0_attn_Wv, L0_attn_Wo, L0_attn_Wg, L0_attn_bg, L0_attn_Wog, L0_ffn_gate_w, L0_ffn_gate_bias, L0_ffn_w_gate, L0_ffn_w_up, L0_ffn_w_down):

    def _L0_attn_ref(x, Wq, Wk, Wv, Wo, Wg, bg, Wog):
        import jax, jax.numpy as jnp
        from jax import lax
        import numpy as np
        DIM = 256
        H = 8
        DK = 128
        DV = 64
        GATE_NORM = 16.0

        def _gla(x, Wq, Wk, Wv, Wo, Wg, bg, Wog):
            B, S, D = x.shape
            q = (x @ Wq).reshape(B, S, H, DK)
            k = (x @ Wk).reshape(B, S, H, DK) * DK ** (-0.5)
            v = (x @ Wv).reshape(B, S, H, DV)
            alpha = jax.nn.sigmoid((x @ Wg + bg) / GATE_NORM)

            def step(state, inp):
                qt, kt, vt, at = inp
                state = at[..., None, None] * state + kt[..., None] * vt[:, :, None, :]
                out_t = jnp.einsum('bhk,bhkv->bhv', qt, state)
                return (state, out_t)
            state0 = jnp.zeros((B, H, DK, DV), x.dtype)
            xs = (jnp.moveaxis(q, 1, 0), jnp.moveaxis(k, 1, 0), jnp.moveaxis(v, 1, 0), jnp.moveaxis(alpha, 1, 0))
            _, outs = lax.scan(step, state0, xs)
            out = jnp.moveaxis(outs, 0, 1).reshape(B, S, H * DV)
            og = jax.nn.sigmoid(x @ Wog)
            return out * og @ Wo
        return _gla(x, Wq, Wk, Wv, Wo, Wg, bg, Wog)

    def _L0_ffn_ref(hidden_states, gate_w, gate_bias, w_gate, w_up, w_down):
        import jax, jax.numpy as jnp
        import numpy as np
        B, S, H, I = (2, 512, 256, 128)
        E, K, G, TG = (64, 8, 8, 4)
        SCALE = 2.5
        CAP = 256
        b, s, h = hidden_states.shape
        x = hidden_states.reshape(-1, h)
        n = x.shape[0]
        logits = x.astype(jnp.float32) @ gate_w.astype(jnp.float32).T
        scores = jax.nn.sigmoid(logits)
        sfc = scores + gate_bias[None, :]
        group_scores = jax.lax.top_k(sfc.reshape(n, G, E // G), 2)[0].sum(-1)
        gidx = jax.lax.top_k(group_scores, TG)[1]
        gmask = jnp.zeros((n, G), bool).at[jnp.arange(n)[:, None], gidx].set(True)
        smask = jnp.repeat(gmask, E // G, axis=1)
        tmp = jnp.where(smask, sfc, -jnp.inf)
        topk_idx = jax.lax.top_k(tmp, K)[1]
        topk_w = jnp.take_along_axis(scores, topk_idx, axis=1)
        topk_w = topk_w / (topk_w.sum(-1, keepdims=True) + 1e-20)
        topk_w = topk_w * SCALE
        e = topk_idx.reshape(-1)
        token = jnp.repeat(jnp.arange(n), K)
        oh = jax.nn.one_hot(e, E, dtype=jnp.int32)
        pos = jnp.take_along_axis(jnp.cumsum(oh, 0) - 1, e[:, None], 1)[:, 0]
        valid = pos < CAP
        pos_c = jnp.where(valid, pos, CAP)
        buf = jnp.zeros((E, CAP + 1, h), x.dtype).at[e, pos_c].set(x[token])[:, :CAP]
        g = jnp.einsum('ech,ehi->eci', buf, w_gate)
        u = jnp.einsum('ech,ehi->eci', buf, w_up)
        y = jnp.einsum('eci,eih->ech', jax.nn.silu(g) * u, w_down)
        y_slots = y[e, jnp.minimum(pos, CAP - 1)]
        w_slot = topk_w.reshape(-1) * valid.astype(topk_w.dtype)
        out = jnp.zeros((n, h), jnp.float32).at[token].add(y_slots * w_slot[:, None])
        return out.reshape(b, s, h)
    x = L0_attn_x
    xn = _layernorm(x, axis=-1)
    x = x + _L0_attn_ref(xn, L0_attn_Wq, L0_attn_Wk, L0_attn_Wv, L0_attn_Wo, L0_attn_Wg, L0_attn_bg, L0_attn_Wog) + _L0_ffn_ref(xn, L0_ffn_gate_w, L0_ffn_gate_bias, L0_ffn_w_gate, L0_ffn_w_up, L0_ffn_w_down)
    return x

_drawn_inputs = setup_inputs


def setup_inputs(seed=0):
    import zlib

    import numpy as np

    out = dict(_drawn_inputs(seed))
    spreads = {'L0_attn_bg': (0.0, 0.8)}
    factors = {'L0_attn_Wq': 8.0,
     'L0_attn_Wk': 8.0,
     'L0_attn_Wv': 8.0,
     'L0_attn_Wo': 8.0,
     'L0_attn_Wg': 8.0,
     'L0_attn_Wog': 8.0}
    for name, (base, spread) in spreads.items():
        noise = np.random.default_rng([zlib.crc32(name.encode()), seed]).standard_normal(out[name].shape)
        drawn = base * np.exp(spread * noise) if base else spread * noise
        out[name] = jnp.asarray(drawn.astype(out[name].dtype))
    for name, factor in factors.items():
        out[name] = (out[name] * factor).astype(out[name].dtype)
    return out
```

```python
from contextlib import ExitStack

import concourse.bass as bass
from concourse import mybir

F32 = mybir.dt.float32
BF16 = mybir.dt.bfloat16
U32 = mybir.dt.uint32
ALU = mybir.AluOpType
ACT = mybir.ActivationFunctionType
AX = mybir.AxisListType

P = 128
B, S, D = 4, 2048, 256
H, DK, DV = 8, 128, 64
HV = H * DV
KD = D // P
KO = HV // P
N = B * S
C = S // P
T = N // P
BP = B * P
E, I, G, TG, K = 64, 128, 8, 4, 8
EG = E // G
CAP = 256
NHALF = CAP // P
SCALE_OUT = 2.5
GATE_NORM = 16.0
NR = E + H
XW = D + E
ROWS = N + CAP
BIG = 3.0e38
TAKEN = 3.3e38
STEP_E = H
E_STEPS = E // STEP_E
N_CONSTS = 13
EB = 4
CNT_G = E // EB
NORM_CHAIN, ROUTE_CHAIN = 3, 20


def at(c, per, k):
    return c * per + k


def build(nc, x_in, Wq, Wk, Wv, Wo, Wg, bg, Wog, gate_w, gate_bias, w_gate, w_up, w_down, out):
    with ExitStack() as ctx:
        def sb(name, shape, dt=F32):
            return ctx.enter_context(nc.sbuf_tensor(name, shape, dt))

        def sem(name):
            return ctx.enter_context(nc.semaphore(name))

        xT_dram = nc.dram_tensor("xT_dram", (C, P, KD * BP), F32).ap()
        table = nc.dram_tensor("table", (ROWS, XW), F32).ap()
        decay_dram = nc.dram_tensor("decay_dram", (C, B * H, P), F32).ap()
        acc = nc.dram_tensor("acc", (ROWS, D), F32).ap()

        bank = [ctx.enter_context(nc.psum_tensor(f"bank{i}", [P, 512], F32)) for i in range(8)]

        ident = sb("ident", [P, P])
        eye_heads = sb("eye_heads", [P, H, P])
        upper = sb("upper", [P, P], BF16)
        before = sb("before", [T, T])
        last_row = sb("last_row", [P, P])
        slot_row = sb("slot_row", [T, CAP])
        slot_col = sb("slot_col", [P, NHALF])
        trash_col = sb("trash_col", [P, NHALF])
        tile_one = sb("tile_one", [T, 2])
        wq = sb("wq", [P, KD, H * DK])
        wk = sb("wk", [P, KD, H * DK])
        wv = sb("wv", [P, KD, HV])
        wog = sb("wog", [P, KD, HV])
        wo = sb("wo", [P, KO, D])

        cum_all = sb("cum_all", [P, C, B, H])
        last_all = sb("last_all", [P, C, B, H])
        sel_all = sb("sel_all", [P, E, B, C], BF16)
        idx_all = sb("idx_all", [P, E + 2, NHALF], U32)
        kept = sb("kept", [P, E_STEPS, B, D])

        xs = sb("xs", [P, KD, BP])
        decay = sb("decay", [P, B, H * P])
        Dt = sb("Dt", [P, B, H, P])
        qT = sb("qT", [P, 2, BP])
        kT = sb("kT", [P, 2, BP])
        kw = sb("kw", [P, B, DK])
        At = sb("At", [P, B, P])
        V = sb("V", [P, B, HV])
        og = sb("og", [P, B, HV])
        t1 = sb("t1", [P, B, HV])
        gated = sb("gated", [P, B, HV])
        oT = sb("oT", [P, HV])
        state = sb("state", [P, H, B, DV])

        ARENA = 6656
        arena = sb("arena", [P, ARENA])
        used = {}

        def view(phase, shape, dt=F32):
            words = 1
            for n in shape[1:]:
                words *= n
            lo = used.get(phase, 0)
            used[phase] = lo + words
            assert used[phase] <= ARENA, phase
            a = arena[0:shape[0], lo:lo + words]
            if dt is not F32:
                a = a.bitcast(dt)
            if len(shape) == 3:
                a = a.rearrange("p (a b) -> p a b", a=shape[1])
            if len(shape) == 4:
                a = a.rearrange("p (a b c) -> p a b c", a=shape[1], b=shape[2])
            return a

        xt = view(1, [P, B, D])
        xn = view(1, [P, B, D])
        xnT = view(1, [P, KD, BP])
        wr = view(1, [P, KD, NR])
        gw_rows = view(1, [E, D])
        bias_e = view(1, [P, E])
        bias_g = view(1, [P, H])
        below = view(1, [P, G, G])
        above = view(1, [P, G, G])
        stats = view(1, [P, B, 6])
        mv = view(1, [P, B, 2])
        std = view(1, [P, B])
        rstd = view(1, [P, B])
        score = view(1, [P, B, E])
        zg = view(1, [P, B, H])
        alpha = view(1, [P, B, H])
        alphaT = view(1, [B * H, P])
        cumT = view(1, [B * H, P])
        zeros_t = view(1, [B * H, P])
        cum_c = view(1, [P, B * H])
        sfc = view(1, [P, B * G, EG])
        hi1 = view(1, [P, B * G, 4])
        lo1 = view(1, [P, B * G, 4])
        hi2 = view(1, [P, B * G, 2])
        lo2 = view(1, [P, B * G, 2])
        mid = view(1, [P, B * G, 2])
        hi3 = view(1, [P, B * G, 1])
        lo3 = view(1, [P, B * G, 1])
        gsc = view(1, [P, B, G])
        gt = view(1, [P, B * G, G])
        rank = view(1, [P, B * G])
        masked = view(1, [P, B, E])
        top8 = view(1, [P, B, K])
        left = gt.rearrange("p a b -> p (a b)").rearrange("p (b e) -> p b e", b=B)
        chosen = view(1, [P, B, E])
        total = view(1, [P, B])
        inv = view(1, [P, B])
        weight = view(1, [P, B, E])
        ge = view(1, [P, B * G, G])

        counts = kept[0:T, :, :, :].rearrange("p s b d -> p (s b d)").rearrange("p (e t) -> p e t", e=E)
        sel_cur = sb("sel_cur", [P, EB, T], BF16)
        firsts = view(2, [T, E])
        ends = view(2, [T, E])
        hot = view(2, [T, 2, CAP])
        hot0 = view(2, [T, 2, CAP])
        junk = view(2, [P, NHALF, P])
        cnt = view(2, [P, E, NHALF])
        bv = view(2, [P, E, NHALF, 2])
        slot_tok = view(2, [P, E, NHALF])

        idx = sb("idx", [P, 4, NHALF], U32)
        xg = view(3, [P, 2, NHALF, XW])
        xgT = view(3, [P, KD, CAP])
        wge = view(3, [P, 2, KD, I])
        wue = view(3, [P, 2, KD, I])
        wde = view(3, [P, 2, D])
        sg = view(3, [P, CAP])
        hs = view(3, [P, CAP])
        hT = view(3, [P, CAP])
        yb = view(3, [P, 2, NHALF, D])

        res = view(4, [P, B, D])
        acc_new = view(4, [P, B, D])
        acc_old = view(4, [P, B, D])

        x_tiles = x_in.rearrange("b (c p) d -> c p b d", p=P)
        out_tiles = out.rearrange("b (c p) d -> c p b d", p=P)
        acc_tiles = acc[0:N, :].rearrange("(b c p) d -> c p b d", b=B, c=C)
        acc_init = acc[0:N, :].rearrange("(b s) d -> b s d", b=B)
        tab_tiles = table[0:N, :].rearrange("(b c p) w -> c p b w", b=B, c=C)

        w_in, w_const, w_ident, consts = sem("w_in"), sem("w_const"), sem("w_ident"), sem("consts")
        gwT_ps, gwT_cp = sem("gwT_ps"), sem("gwT_cp")
        init_acc, zero_rows = sem("init_acc"), sem("zero_rows")
        x_loaded = sem("x_loaded")
        mv_ready, std_ready, xn_ready = sem("mv_ready"), sem("std_ready"), sem("xn_ready")
        xn_stored, xT_stored, wt_stored, dec_stored = (sem("xn_stored"), sem("xT_stored"), sem("wt_stored"),
                                                       sem("dec_stored"))
        xT_ps, xT_cp, lg_ps = sem("xT_ps"), sem("xT_cp"), sem("lg_ps")
        score_ready, zg_ready, alpha_ready = sem("score_ready"), sem("zg_ready"), sem("alpha_ready")
        aT_ps, aT_cp, cumT_ready, cum_ps, cum_cp = (sem("aT_ps"), sem("aT_cp"), sem("cumT_ready"), sem("cum_ps"),
                                                    sem("cum_cp"))
        dec_ready, last_ps, last_cp = sem("dec_ready"), sem("last_ps"), sem("last_cp")
        weight_ready, sel_kept = sem("weight_ready"), sem("sel_kept")
        norm_chain, route_chain = sem("norm_chain"), sem("route_chain")
        selc_ready, cnt_ps, cnt_cp, first_ps, first_cp = (sem("selc_ready"), sem("cnt_ps"), sem("cnt_cp"),
                                                          sem("first_ps"), sem("first_cp"))
        tab_chain, hot_half, hot_ready, tok_ps, tok_cnt, tok_bv, idx_ready = (
            sem("tab_chain"), sem("hot_half"), sem("hot_ready"), sem("tok_ps"), sem("tok_cnt"), sem("tok_bv"),
            sem("idx_ready"))
        xs_in, dec_in = sem("xs_in"), sem("dec_in")
        qk_ps, qk_cp = sem("qk_ps"), sem("qk_cp")
        v_ps, v_cp, og_ps, og_cp = sem("v_ps"), sem("v_cp"), sem("og_ps"), sem("og_cp")
        kt_ps, kw_cp, s_ps, a_cp = sem("kt_ps"), sem("kw_cp"), sem("s_ps"), sem("a_cp")
        oi_ps, oi_cp, u_ps, state_up = sem("oi_ps"), sem("oi_cp"), sem("u_ps"), sem("state_up")
        ot_ps, ot_cp, wo_ps, wo_cp = sem("ot_ps"), sem("ot_cp"), sem("wo_ps"), sem("wo_cp")
        scan_done, part_done, gate_done = sem("scan_done"), sem("part_done"), sem("gate_done")
        state_zero = sem("state_zero")
        gathered = [sem("gathered0"), sem("gathered1")]
        ew_in = [sem("ew_in0"), sem("ew_in1")]
        idx_cp, scattered = sem("idx_cp"), sem("scattered")
        xg_ps, xg_cp, gu_ps, sg_ready, hs_ready, h_ready, y_ps, y_cp = (
            sem("xg_ps"), sem("xg_cp"), sem("gu_ps"), sem("sg_ready"), sem("hs_ready"), sem("h_ready"), sem("y_ps"),
            sem("y_cp"))
        accn_in, acco_in, old_ready, out_new, out_old = (
            sem("accn_in"), sem("acco_in"), sem("old_ready"), sem("out_new"), sem("out_old"))

        def wait_apart(eng, semaphore, value):
            if not isinstance(value, int):
                value = eng.snap(eng.to_reg(value))
            eng.wait_ge(consts, N_CONSTS)
            eng.wait_ge(semaphore, value)

        def wait_past(eng, semaphore, value):
            if not isinstance(value, int) or value > 0:
                eng.wait_ge(semaphore, value)

        block = ctx.enter_context(nc.Block())

        @block.sync
        def _(sp):
            sp.dma_start(gw_rows, gate_w).then_inc(w_const, 16)
            sp.dma_start(bias_e, gate_bias.rearrange("(a e) -> a e", a=1).broadcast_to([P, E])).then_inc(w_const, 16)
            sp.dma_start(bias_g, bg.rearrange("(a e) -> a e", a=1).broadcast_to([P, H])).then_inc(w_const, 16)
            sp.dma_start(wr[:, :, E:NR], Wg.rearrange("(k p) n -> p k n", k=KD)).then_inc(w_const, 16)
            def chunk(c):
                wait_past(sp, xn_ready, c)
                sp.dma_start(xt, x_tiles[c]).then_inc(x_loaded, 16)
                sp.wait_ge(xn_ready, c + 1)
                sp.dma_start(tab_tiles[c][:, :, 0:D], xn).then_inc(xn_stored, 16)
                sp.wait_ge(xT_cp, c + 1)
                sp.dma_start(xT_dram[c], xnT.rearrange("p k n -> p (k n)")).then_inc(xT_stored, 16)

            chunk(0)
            with sp.Fori(1, C) as c:
                chunk(c)
            for w, src, k in ((wq, Wq, KD), (wk, Wk, KD), (wv, Wv, KD), (wog, Wog, KD), (wo, Wo, KO)):
                sp.dma_start(w[:, :, :], src.rearrange("(k p) n -> p k n", k=k)).then_inc(w_in, 16)
            for b in range(B):
                sp.dma_start(acc_init[b], x_in[b]).then_inc(init_acc, 16)

            def load_xs(c):
                sp.dma_start(xs[:, :, :].rearrange("p k n -> p (k n)"), xT_dram[c]).then_inc(xs_in, 16)

            def load_decay(c):
                src = decay_dram[c].rearrange("(a r) t -> a (r t)", a=1).broadcast_to([P, B * H * P])
                sp.dma_start(decay[:, :, :].rearrange("p b n -> p (b n)"), src).then_inc(dec_in, 16)

            def load_expert(e, slot):
                sp.dma_start(wge[:, slot], w_gate[e].rearrange("(k p) i -> p k i", k=KD)).then_inc(ew_in[slot], 16)
                sp.dma_start(wue[:, slot], w_up[e].rearrange("(k p) i -> p k i", k=KD)).then_inc(ew_in[slot], 16)
                sp.dma_start(wde[:, slot], w_down[e]).then_inc(ew_in[slot], 16)

            def step(c, n_experts, ahead=True):
                if ahead:
                    sp.wait_ge(scan_done, 4 * (c + 1))
                    load_decay(c + 1)
                for j in range(n_experts):
                    e = (c - 1) * STEP_E + j
                    sp.wait_ge(y_ps, e + 1)
                    load_expert(e + 2, j % 2)
                if ahead:
                    sp.wait_ge(og_ps, 4 * (c + 1))
                    load_xs(c + 1)

            sp.wait_ge(xT_stored, 16 * C)
            load_xs(0)
            sp.wait_ge(dec_stored, 16 * C)
            load_decay(0)
            sp.wait_ge(idx_ready, 1)
            load_expert(0, 0)
            load_expert(1, 1)
            step(0, 0)
            with sp.Fori(1, E_STEPS) as c:
                step(c, STEP_E)
            step(E_STEPS, STEP_E - 2)

            def final_loads(c):
                sp.wait_ge(wo_cp, 4 * (c - 1))
                wait_past(sp, out_new, 16 * (c - 1 - E_STEPS))
                sp.dma_start(acc_new, acc_tiles[c - 1]).then_inc(accn_in, 16)
                wait_past(sp, out_old, 16 * (c - 1 - E_STEPS))
                sp.dma_start(acc_old, acc_tiles[c - 1 - E_STEPS]).then_inc(acco_in, 16)

            def final_stores(c):
                wait_apart(sp, old_ready, c - E_STEPS)
                sp.dma_start(out_tiles[c - 1 - E_STEPS], acc_old).then_inc(out_old, 16)
                sp.wait_ge(wo_cp, 4 * c)
                sp.dma_start(out_tiles[c - 1], res).then_inc(out_new, 16)

            sp.wait_ge(scattered, 16 * NHALF * E)
            for slot in range(2):
                sp.wait_ge(gathered[slot], 16 * NHALF * (E // 2 + 1))
            final_loads(E_STEPS + 1)
            step(E_STEPS + 1, 0)
            final_stores(E_STEPS + 1)
            with sp.Fori(E_STEPS + 2, C - 1) as c:
                final_loads(c)
                step(c, 0)
                final_stores(c)
            final_loads(C - 1)
            step(C - 1, 0, ahead=False)
            final_stores(C - 1)
            final_loads(C)
            final_stores(C)
            sp.wait_ge(out_old, 16 * E_STEPS)
            sp.wait_ge(out_new, 16 * (C - E_STEPS))

        @block.gpsimd
        def _(pool):
            for m in (ident[:, :], last_row[:, :], upper[:, :], before[:, :]):
                pool.memset(m, 1.0).then_inc(w_ident, 1)
            pool.memset(eye_heads[:, :, :], 1.0).then_inc(w_ident, 1)
            pool.memset(below, 1.0).then_inc(w_ident, 1)
            pool.memset(above, 1.0).then_inc(w_ident, 1)
            zeros = kept[:, 0, :, :].rearrange("p b d -> p (b d)")[:, 0:XW]
            pool.memset(zeros, 0.0).then_inc(w_ident, 1)
            pool.wait_ge(w_ident, 8)
            pool.affine_select(out=ident[:, :], in_=ident[:, :], compare_op=ALU.is_equal, fill=0.0, base=0,
                               pattern=[[-1, P]], channel_multiplier=1).then_inc(consts, 1)
            pool.affine_select(out=last_row[:, :], in_=last_row[:, :], compare_op=ALU.is_equal, fill=0.0,
                               base=-(P - 1), pattern=[[0, P]], channel_multiplier=1).then_inc(consts, 1)
            pool.affine_select(out=upper[:, :], in_=upper[:, :], compare_op=ALU.is_ge, fill=0.0, base=0,
                               pattern=[[1, P]], channel_multiplier=-1).then_inc(consts, 1)
            pool.affine_select(out=before[:, :], in_=before[:, :], compare_op=ALU.is_gt, fill=0.0, base=0,
                               pattern=[[1, T]], channel_multiplier=-1).then_inc(consts, 1)
            pool.affine_select(out=eye_heads[:, :, :], in_=eye_heads[:, :, :], compare_op=ALU.is_equal, fill=0.0,
                               base=0, pattern=[[0, H], [-1, P]], channel_multiplier=1).then_inc(consts, 1)
            pool.affine_select(out=below, in_=below, compare_op=ALU.is_gt, fill=0.0, base=0,
                               pattern=[[1, G], [-1, G]], channel_multiplier=0).then_inc(consts, 1)
            pool.affine_select(out=above, in_=above, compare_op=ALU.is_gt, fill=0.0, base=0,
                               pattern=[[-1, G], [1, G]], channel_multiplier=0).then_inc(consts, 1)
            f = dict(allow_small_or_imprecise_dtypes=True)
            pool.iota(slot_row[:, :], [[1, CAP]], base=0, channel_multiplier=0, **f).then_inc(consts, 1)
            pool.iota(slot_col[:, :], [[P, NHALF]], base=0, channel_multiplier=1, **f).then_inc(consts, 1)
            pool.iota(trash_col[:, :], [[P, NHALF]], base=N, channel_multiplier=1, **f).then_inc(consts, 1)
            pool.iota(tile_one[:, 0:1], [[0, 1]], base=0, channel_multiplier=P, **f).then_inc(consts, 1)
            pool.memset(tile_one[:, 1:2], 1.0).then_inc(consts, 1)
            pool.memset(state[:, :, :, :], 0.0).then_inc(state_zero, 1)
            pool.memset(zeros_t, 0.0).then_inc(consts, 1)
            for j in range(NHALF):
                rows = slice(N + j * P, N + (j + 1) * P)
                pool.dma_start(table[rows, :], zeros).then_inc(zero_rows, 16)
                pool.dma_start(acc[rows, :], zeros[:, 0:D]).then_inc(zero_rows, 16)
            pool.wait_ge(zero_rows, 16 * 2 * NHALF)

            with pool.Fori(0, C) as c:
                pool.wait_ge(dec_ready, c + 1)
                pool.dma_start(decay_dram[c], alphaT).then_inc(dec_stored, 16)
                pool.wait_ge(weight_ready, c + 1)
                pool.dma_start(tab_tiles[c][:, :, D:XW], weight).then_inc(wt_stored, 16)
                pool.tensor_copy(sel_all[:, :, :, c].rearrange("p e b -> p b e"), chosen).then_inc(sel_kept, 1)

            def gather(e, u):
                pool.tensor_copy(idx[:, u % 4, :], idx_all[:, e, :]).then_inc(idx_cp, 1)
                wait_apart(pool, idx_cp, e + 1)
                for j in range(NHALF):
                    pool.indirect_dma_start(
                        out=xg[:, u % 2, j, :], out_offset=None, in_=table[:, :],
                        in_offset=bass.IndirectOffsetOnAxis(ap=idx[:, u % 4, j:j + 1], axis=0),
                        bounds_check=ROWS - 1, oob_is_err=True).then_inc(gathered[u % 2], 16)

            def scatter(e, u, j):
                if not isinstance(e, int) or e + j > 0:
                    wait_apart(pool, scattered, 16 * (NHALF * e + j))
                pool.indirect_dma_start(
                    out=acc[:, :], out_offset=bass.IndirectOffsetOnAxis(ap=idx[:, u % 4, j:j + 1], axis=0),
                    in_=yb[:, u % 2, j, :], in_offset=None, bounds_check=ROWS - 1, oob_is_err=True,
                    compute_op=ALU.add).then_inc(scattered, 16)

            pool.wait_ge(idx_ready, 1)
            pool.wait_ge(wt_stored, 16 * C)
            pool.wait_ge(xn_stored, 16 * C)
            gather(0, 0)
            gather(1, 1)
            pool.wait_ge(init_acc, 16 * B)
            def four_experts(i):
                for u in range(4):
                    e = 4 * i + u
                    pool.wait_ge(y_cp, e + 1)
                    scatter(e, u, 0)
                    gather(e + 2, u + 2)
                    scatter(e, u, 1)

            four_experts(0)
            with pool.Fori(1, E // 4) as i:
                four_experts(i)

        @block.tensor
        def _(pe):
            mm, tr = pe.matmul, pe.transpose
            pe.wait_ge(consts, N_CONSTS)
            pe.wait_ge(w_const, 64)
            for k in range(KD):
                last = tr(bank[0][:, k * E:(k + 1) * E], gw_rows[:, k * P:(k + 1) * P], ident[0:E, 0:E])
            last.then_inc(gwT_ps, 1)
            pe.wait_ge(gwT_cp, 1)

            def decay_part(c):
                pe.wait_ge(alpha_ready, c + 1)
                tr(bank[3][0:B * H, 0:P], alpha.rearrange("p b h -> p (b h)"), ident[:, :]).then_inc(aT_ps, 1)
                wait_apart(pe, cumT_ready, c + 1)
                tr(bank[4][:, 0:B * H], cumT, ident[0:B * H, 0:B * H]).then_inc(cum_ps, 1)
                pe.wait_ge(cum_cp, c + 1)
                mm(bank[5][:, 0:B * H], last_row[:, :], cum_c, start=True, stop=True).then_inc(last_ps, 1)

            def front(c):
                pe.wait_ge(xn_ready, c + 1)
                for k in range(KD):
                    for b in range(B):
                        last = tr(bank[k][:, b * P:(b + 1) * P], xn[:, b, k * P:(k + 1) * P], ident[:, :])
                last.then_inc(xT_ps, 1)
                pe.wait_ge(xT_cp, c + 1)
                for b in range(B):
                    for k in range(KD):
                        last = mm(bank[2][:, b * NR:(b + 1) * NR], xnT[:, k, b * P:(b + 1) * P], wr[:, k, :],
                                  start=(k == 0), stop=(k == KD - 1))
                last.then_inc(lg_ps, 1)

            front(0)
            with pe.Fori(1, C) as c:
                decay_part(c - 1)
                front(c)
            decay_part(C - 1)

            pe.wait_ge(last_cp, C)
            def count_group(g):
                pe.wait_ge(selc_ready, g + 1)
                wait_past(pe, cnt_cp, g)
                for j in range(EB):
                    last = mm(bank[0][0:T, j * P:(j + 1) * P], sel_cur[:, j, :], upper[:, :], start=True, stop=True)
                last.then_inc(cnt_ps, 1)

            count_group(0)
            with pe.Fori(1, CNT_G) as g:
                count_group(g)
            pe.wait_ge(cnt_cp, CNT_G)
            mm(bank[2][0:T, 0:E], before[:, :], counts[:, :, P - 1], start=True, stop=True).then_inc(first_ps, 1)
            pe.wait_ge(first_cp, 1)
            def slots_of_two(i):
                for u in range(2):
                    e = 2 * i + u
                    pe.wait_ge(hot_ready, e + 1)
                    wait_past(pe, tok_bv, e)
                    for j in range(NHALF):
                        lhs = hot[:, u, j * P:(j + 1) * P]
                        mm(bank[3 + u][:, j * P:(j + 1) * P], lhs, counts[:, e, :], start=True, stop=True)
                        last = mm(bank[3 + u][:, 256 + 2 * j:258 + 2 * j], lhs, tile_one[:, :], start=True,
                                  stop=True)
                    last.then_inc(tok_ps, 1)

            slots_of_two(0)
            with pe.Fori(1, E // 2) as i:
                slots_of_two(i)

            def proj_qk(c, h, which):
                u = 2 * h + which
                w = (wq, wk)[which]
                if not (isinstance(c, int) and at(c, 16, u) < 2):
                    pe.wait_ge(qk_cp, at(c, 16, u) - 1)
                for k in range(KD):
                    last = mm(bank[which][:, :], w[:, k, h * DK:(h + 1) * DK], xs[:, k, :], start=(k == 0),
                              stop=(k == KD - 1))
                last.then_inc(qk_ps, 1)

            def bank4_free(c, item, b):
                first = isinstance(c, int) and c == 0
                if item == "v" and b == 0:
                    if not first:
                        pe.wait_ge(og_cp, 4 * c)
                elif item == "v":
                    pe.wait_ge(v_cp, 4 * c + b)
                elif item == "og" and b == 0:
                    pe.wait_ge(v_cp, 4 * c + 4)
                elif item == "og" and (b < 3 or first):
                    pe.wait_ge(og_cp, 4 * c + b)
                elif item == "og":
                    pe.wait_ge(wo_cp, 4 * c)
                elif item == "wo" and b == 0:
                    pe.wait_ge(og_cp, 4 * c + 3 if not (isinstance(c, int) and c == C) else 4 * c)
                else:
                    pe.wait_ge(wo_cp, 4 * (c - 1) + b)

            def proj_tok(c, item, b):
                w, ready = {"v": (wv, v_ps), "og": (wog, og_ps)}[item]
                bank4_free(c, item, b)
                for k in range(KD):
                    last = mm(bank[4][:, :], xs[:, k, b * P:(b + 1) * P], w[:, k, :], start=(k == 0),
                              stop=(k == KD - 1))
                last.then_inc(ready, 1)

            def keys_back(c, h):
                pe.wait_ge(qk_cp, at(c, 16, 2 * h + 2))
                if 5 <= h + 1 <= 8 and not (isinstance(c, int) and c == 0):
                    pe.wait_ge(ot_cp, 4 * (c - 1) + h - 3)
                elif not (isinstance(c, int) and c == 0 and h == 0):
                    pe.wait_ge(kw_cp, at(c, 8, h))
                for b in range(B):
                    last = tr(bank[3][:, b * P:(b + 1) * P], kT[:, h % 2, b * P:(b + 1) * P], ident[:, :])
                last.then_inc(kt_ps, 1)

            def scores(c, h):
                if not (isinstance(c, int) and c == 0 and h == 0):
                    pe.wait_ge(a_cp, at(c, 8, h))
                for b in range(B):
                    last = mm(bank[2][:, b * P:(b + 1) * P], kT[:, h % 2, b * P:(b + 1) * P],
                              qT[:, h % 2, b * P:(b + 1) * P], start=True, stop=True)
                last.then_inc(s_ps, 1)

            def outputs(c, h):
                pe.wait_ge(a_cp, at(c, 8, h + 1))
                pe.wait_ge(v_cp, 4 * c + 4)
                if not (isinstance(c, int) and c == 0 and h == 0):
                    pe.wait_ge(oi_cp, at(c, 8, h))
                for b in range(B):
                    mm(bank[5][:, b * DV:(b + 1) * DV], At[:, b, :], V[:, b, h * DV:(h + 1) * DV], start=True,
                       stop=True)
                if isinstance(c, int) and c == 0:
                    pe.wait_ge(state_zero, 1)
                else:
                    pe.wait_ge(state_up, at(c - 1, 8, h + 1))
                for b in range(B):
                    last = mm(bank[5][:, 256 + b * DV:256 + (b + 1) * DV], qT[:, h % 2, b * P:(b + 1) * P],
                              state[:, h, b, :], start=True, stop=True)
                last.then_inc(oi_ps, 1)

            def update(c, h):
                pe.wait_ge(kw_cp, at(c, 8, h + 1))
                if not (isinstance(c, int) and c == 0 and h == 0):
                    pe.wait_ge(state_up, at(c, 8, h))
                for b in range(B):
                    last = mm(bank[6][:, b * DV:(b + 1) * DV], kw[:, b, :], V[:, b, h * DV:(h + 1) * DV],
                              start=True, stop=True)
                last.then_inc(u_ps, 1)

            def outs_back(c, b):
                pe.wait_ge(gate_done, 4 * (c - 1) + b + 1)
                if isinstance(c, int) and c == C:
                    if b == 0:
                        pe.wait_ge(kw_cp, 8 * C)
                    else:
                        pe.wait_ge(ot_cp, 4 * (c - 1) + b)
                else:
                    pe.wait_ge(kw_cp, at(c, 8, b + 4))
                for j in range(KO):
                    last = tr(bank[3][:, j * P:(j + 1) * P], gated[:, b, j * P:(j + 1) * P], ident[:, :])
                last.then_inc(ot_ps, 1)

            def out_proj(c, b):
                bank4_free(c, "wo", b)
                pe.wait_ge(ot_cp, 4 * (c - 1) + b + 1)
                for j in range(KO):
                    last = mm(bank[4][:, 0:D], oT[:, j * P:(j + 1) * P], wo[:, j, :], start=(j == 0),
                              stop=(j == KO - 1))
                last.then_inc(wo_ps, 1)

            def expert_tokens(c, j):
                e = (c - 1) * STEP_E + j
                pe.wait_ge(gathered[j % 2], ((c - 1) * (STEP_E // 2) + j // 2 + 1) * 16 * NHALF)
                if j > 0:
                    pe.wait_ge(y_cp, e)
                else:
                    pe.wait_ge(gate_done, 4 * (c - 1) + 1)
                for k in range(KD):
                    for half in range(NHALF):
                        lo = k * CAP + half * P
                        last = tr(bank[7][:, lo:lo + P], xg[:, j % 2, half, k * P:(k + 1) * P], ident[:, :])
                last.then_inc(xg_ps, 1)

            def expert_hidden(c, j):
                e = (c - 1) * STEP_E + j
                pe.wait_ge(ew_in[j % 2], ((c - 1) * (STEP_E // 2) + j // 2 + 1) * 48)
                pe.wait_ge(xg_cp, e + 1)
                for m, w in enumerate((wge, wue)):
                    for k in range(KD):
                        last = mm(bank[7][:, m * CAP:(m + 1) * CAP], w[:, j % 2, k, :], xgT[:, k, :],
                                  start=(k == 0), stop=(k == KD - 1))
                last.then_inc(gu_ps, 1)

            def expert_down(c, j):
                e = (c - 1) * STEP_E + j
                pe.wait_ge(h_ready, e + 1)
                for half in range(NHALF):
                    last = mm(bank[7][:, half * D:(half + 1) * D], hT[:, half * P:(half + 1) * P],
                              wde[:, j % 2, :], start=True, stop=True)
                last.then_inc(y_ps, 1)

            def step(c, experts):
                first = isinstance(c, int) and c == 0
                pe.wait_ge(xs_in, 16 * (c + 1))
                proj_tok(c, "v", 0)
                proj_qk(c, 0, 0)
                proj_tok(c, "v", 1)
                proj_qk(c, 0, 1)
                proj_tok(c, "v", 2)
                proj_tok(c, "v", 3)
                for s in range(1, H + 1):
                    if experts:
                        expert_tokens(c, s - 1)
                    keys_back(c, s - 1)
                    scores(c, s - 1)
                    if s <= 3:
                        proj_tok(c, "og", s - 1)
                    if 4 <= s <= 7 and not first:
                        outs_back(c, s - 4)
                    if s < H:
                        proj_qk(c, s, 0)
                    if experts:
                        expert_hidden(c, s - 1)
                    if 4 <= s <= 7 and not first:
                        out_proj(c, s - 4)
                    if s < H:
                        proj_qk(c, s, 1)
                    else:
                        proj_tok(c, "og", 3)
                    outputs(c, s - 1)
                    update(c, s - 1)
                    if experts:
                        expert_down(c, s - 1)

            pe.wait_ge(tok_cnt, E)
            pe.wait_ge(tok_bv, E)
            pe.wait_ge(w_in, 80)
            step(0, False)
            with pe.Fori(1, E_STEPS + 1) as c:
                step(c, True)
            with pe.Fori(E_STEPS + 1, C) as c:
                step(c, False)
            for b in range(B):
                outs_back(C, b)
                out_proj(C, b)

        @block.scalar
        def _(act):
            f = nc.scalar.activation
            act.wait_ge(gwT_ps, 1)
            f(wr[:, :, 0:E], bank[0][:, 0:KD * E].rearrange("p (k e) -> p k e", k=KD), ACT.Copy).then_inc(gwT_cp, 1)

            def std_of(c):
                act.wait_ge(mv_ready, c + 1)
                f(std, mv[:, :, 1], ACT.Sqrt).then_inc(std_ready, 1)

            def sigmoids(c):
                act.wait_ge(zg_ready, c + 1)
                logits = bank[2][:, 0:B * NR].rearrange("p (b n) -> p b n", b=B)
                f(score, logits[:, :, 0:E], ACT.Sigmoid).then_inc(score_ready, 1)
                f(alpha, zg, ACT.Sigmoid, scale=1.0 / GATE_NORM).then_inc(alpha_ready, 1)

            def tokens(c):
                act.wait_ge(xT_ps, c + 1)
                wait_past(act, xT_stored, 16 * c)
                for k in range(KD):
                    ins = f(xnT[:, k, :], bank[k][:, :], ACT.Copy)
                ins.then_inc(xT_cp, 1)

            std_of(0)
            tokens(0)
            with act.Fori(1, C) as c:
                std_of(c)
                sigmoids(c - 1)
                tokens(c)
            sigmoids(C - 1)

            act.wait_ge(sel_kept, C)
            def select_group(g):
                wait_past(act, cnt_ps, g)
                act.copy(sel_cur[:, :, :].rearrange("p j t -> p (j t)"),
                         sel_all[:, bass.ds(g * EB, EB), :, :].rearrange("p e b c -> p (e b c)"))\
                   .then_inc(selc_ready, 1)

            select_group(0)
            with act.Fori(1, CNT_G) as g:
                select_group(g)
            with act.Fori(0, E // 2) as i:
                for u in range(2):
                    e = 2 * i + u
                    act.wait_ge(tok_cnt, e + 1)
                    act.copy(bv[:, e, :, :].rearrange("p a b -> p (a b)"), bank[3 + u][:, 256:260])\
                       .then_inc(tok_bv, 1)

            def qk_copy(c, h, which):
                act.wait_ge(qk_ps, at(c, 16, 2 * h + which + 1))
                dst, scale = ((qT, 1.0), (kT, float(DK) ** -0.5))[which]
                f(dst[:, h % 2, :], bank[which][:, :], ACT.Copy, scale=scale).then_inc(qk_cp, 1)

            def v_copy(c, b):
                act.wait_ge(v_ps, 4 * c + b + 1)
                f(V[:, b, :], bank[4][:, :], ACT.Copy).then_inc(v_cp, 1)

            def og_gate(c, b):
                act.wait_ge(og_ps, 4 * c + b + 1)
                if not (isinstance(c, int) and c == 0):
                    act.wait_ge(gate_done, 4 * (c - 1) + b + 1)
                f(og[:, b, :], bank[4][:, :], ACT.Sigmoid).then_inc(og_cp, 1)

            def outs_copy(c, b):
                act.wait_ge(ot_ps, 4 * (c - 1) + b + 1)
                f(oT[:, :], bank[3][:, :], ACT.Copy).then_inc(ot_cp, 1)

            def expert_tokens(c, j):
                e = (c - 1) * STEP_E + j
                act.wait_ge(xg_ps, e + 1)
                f(xgT.rearrange("p k n -> p (k n)"), bank[7][:, :], ACT.Copy).then_inc(xg_cp, 1)

            def expert_gate(c, j):
                e = (c - 1) * STEP_E + j
                act.wait_ge(gu_ps, e + 1)
                f(sg, bank[7][:, 0:CAP], ACT.Sigmoid).then_inc(sg_ready, 1)

            def step(c, experts):
                first = isinstance(c, int) and c == 0
                v_copy(c, 0)
                qk_copy(c, 0, 0)
                v_copy(c, 1)
                qk_copy(c, 0, 1)
                v_copy(c, 2)
                v_copy(c, 3)
                for s in range(1, H + 1):
                    if experts:
                        expert_tokens(c, s - 1)
                    if s <= 3:
                        og_gate(c, s - 1)
                    if 4 <= s <= 7 and not first:
                        outs_copy(c, s - 4)
                    if s < H:
                        qk_copy(c, s, 0)
                    if experts:
                        expert_gate(c, s - 1)
                    if s < H:
                        qk_copy(c, s, 1)
                    else:
                        og_gate(c, 3)

            step(0, False)
            with act.Fori(1, E_STEPS + 1) as c:
                step(c, True)
            with act.Fori(E_STEPS + 1, C) as c:
                step(c, False)
            for b in range(B):
                outs_copy(C, b)

        @block.vector
        def _(dve):
            tt, ts = dve.tensor_tensor, dve.tensor_scalar

            def chained(semaphore, base):
                n = [0]

                def link(ins, apart=False):
                    n[0] += 1
                    ins.then_inc(semaphore, 1)
                    if apart:
                        wait_apart(dve, semaphore, base + n[0])
                    else:
                        dve.wait_ge(semaphore, base + n[0])
                return link, n

            dve.wait_ge(consts, N_CONSTS)
            dve.wait_ge(w_const, 64)

            def statistics(c):
                dve.wait_ge(x_loaded, 16 * (c + 1))
                link, n = chained(norm_chain, c * NORM_CHAIN)
                for b in range(B):
                    ins = dve.bn_stats(stats[:, b, :], xt[:, b, :])
                link(ins, apart=True)
                for b in range(B):
                    ins = dve.bn_aggr(mv[:, b, :], stats[:, b, :])
                link(ins)
                ts(mv[:, :, 1], mv[:, :, 1], 1e-5, None, ALU.add).then_inc(mv_ready, 1)

            def normalise(c):
                link, n = chained(norm_chain, c * NORM_CHAIN + 2)
                dve.wait_ge(std_ready, c + 1)
                link(dve.reciprocal(rstd, std))
                wait_past(dve, xn_stored, 16 * c)
                wait_past(dve, xT_ps, c)
                for b in range(B):
                    ins = ts(xn[:, b, :], xt[:, b, :], mv[:, b, 0:1], rstd[:, b:b + 1], ALU.subtract, ALU.mult)
                ins.then_inc(xn_ready, 1)

            def gates(c):
                dve.wait_ge(lg_ps, c + 1)
                logits = bank[2][:, 0:B * NR].rearrange("p (b n) -> p b n", b=B)
                tt(zg, logits[:, :, E:NR], bias_g[:, None, :].broadcast_to([P, B, H]), ALU.add).then_inc(zg_ready, 1)

            def decays(c):
                dve.wait_ge(aT_ps, c + 1)
                wait_past(dve, dec_stored, 16 * c)
                dve.tensor_copy(alphaT, bank[3][0:B * H, 0:P]).then_inc(aT_cp, 1)
                dve.wait_ge(aT_cp, c + 1)
                dve.tensor_tensor_scan(cumT, alphaT, zeros_t, 1.0, ALU.mult, ALU.add).then_inc(cumT_ready, 1)
                dve.wait_ge(cumT_ready, c + 1)
                dve.memset(alphaT[:, 0:1], 0.0).then_inc(dec_ready, 1)
                dve.wait_ge(cum_ps, c + 1)
                dve.tensor_copy(cum_c, bank[4][:, 0:B * H]).then_inc(cum_cp, 1)
                dve.tensor_copy(cum_all[:, c, :, :].rearrange("p b h -> p (b h)"), bank[4][:, 0:B * H])
                dve.wait_ge(last_ps, c + 1)
                dve.tensor_copy(last_all[:, c, :, :].rearrange("p b h -> p (b h)"), bank[5][:, 0:B * H])\
                   .then_inc(last_cp, 1)

            def route(c):
                link, n = chained(route_chain, c * ROUTE_CHAIN)
                dve.wait_ge(score_ready, c + 1)
                sfc_t = sfc.rearrange("p a b -> p (a b)").rearrange("p (b e) -> p b e", b=B)
                link(tt(sfc_t, score, bias_e[:, None, :].broadcast_to([P, B, E]), ALU.add))
                tt(hi1, sfc[:, :, 0:4], sfc[:, :, 4:8], ALU.max)
                link(tt(lo1, sfc[:, :, 0:4], sfc[:, :, 4:8], ALU.min))
                tt(mid, hi1[:, :, 0:2], hi1[:, :, 2:4], ALU.min)
                tt(hi2, hi1[:, :, 0:2], hi1[:, :, 2:4], ALU.max)
                link(tt(lo2, lo1[:, :, 0:2], lo1[:, :, 2:4], ALU.max))
                link(tt(lo2, lo2, mid, ALU.max))
                tt(mid[:, :, 0:1], hi2[:, :, 0:1], hi2[:, :, 1:2], ALU.min)
                tt(hi3, hi2[:, :, 0:1], hi2[:, :, 1:2], ALU.max)
                link(tt(lo3, lo2[:, :, 0:1], lo2[:, :, 1:2], ALU.max))
                link(tt(lo3, lo3, mid[:, :, 0:1], ALU.max))
                gsum = gsc.rearrange("p b g -> p (b g)")
                link(tt(gsum[:, :, None], hi3, lo3, ALU.add))
                gt4 = gt.rearrange("p a b -> p (a b)").rearrange("p (b i j) -> p b i j", b=B, i=G)
                ge4 = ge.rearrange("p a b -> p (a b)").rearrange("p (b i j) -> p b i j", b=B, i=G)
                other = gsc[:, :, None, :].broadcast_to([P, B, G, G])
                own = gsc[:, :, :, None].broadcast_to([P, B, G, G])
                tt(gt4, other, own, ALU.is_gt)
                link(tt(ge4, other, own, ALU.is_ge))
                tt(gt4, gt4, above[:, None, :, :].broadcast_to([P, B, G, G]), ALU.mult)
                link(tt(ge4, ge4, below[:, None, :, :].broadcast_to([P, B, G, G]), ALU.mult))
                link(tt(gt4, gt4, ge4, ALU.add))
                link(dve.tensor_reduce(rank, gt, AX.X, ALU.add))
                link(ts(rank, rank, TG - 0.5, -BIG, ALU.is_ge, ALU.mult))
                masked_g = masked.rearrange("p b e -> p (b e)").rearrange("p (a g) -> p a g", g=EG)
                ins = tt(masked_g, sfc, rank[:, :, None].broadcast_to([P, B * G, EG]), ALU.add)
                link(ins, apart=True)
                for b in range(B):
                    ins = dve.max(top8[:, b, :], masked[:, b, :])
                link(ins, apart=True)
                for b in range(B):
                    ins = dve.match_replace(left[:, b, :], top8[:, b, :], masked[:, b, :], -TAKEN)
                link(ins)
                wait_past(dve, sel_kept, c)
                wait_past(dve, wt_stored, 16 * c)
                link(tt(chosen, left, masked, ALU.not_equal))
                link(tt(weight, score, chosen, ALU.mult))
                link(dve.tensor_reduce(total, weight, AX.X, ALU.add))
                link(ts(total, total, 1e-20, None, ALU.add))
                link(dve.reciprocal(inv, total))
                dve.scalar_tensor_tensor(weight, weight, SCALE_OUT, inv[:, :, None].broadcast_to([P, B, E]),
                                         ALU.mult, ALU.mult).then_inc(weight_ready, 1)
                assert n[0] == ROUTE_CHAIN, n

            statistics(0)
            normalise(0)

            def chunk(c):
                statistics(c)
                gates(c - 1)
                normalise(c)
                decays(c - 1)
                route(c - 1)

            chunk(1)
            with dve.Fori(2, C) as c:
                chunk(c)
            gates(C - 1)
            decays(C - 1)
            route(C - 1)

            with dve.Fori(0, CNT_G) as g:
                dve.wait_ge(cnt_ps, g + 1)
                dve.tensor_copy(counts[:, bass.ds(g * EB, EB), :].rearrange("p e t -> p (e t)"), bank[0][0:T, :])\
                   .then_inc(cnt_cp, 1)
            dve.wait_ge(xn_stored, 16 * C)
            dve.wait_ge(xT_stored, 16 * C)
            dve.wait_ge(wt_stored, 16 * C)
            dve.wait_ge(dec_stored, 16 * C)
            dve.wait_ge(sel_kept, C)
            dve.wait_ge(first_ps, 1)
            link, n = chained(tab_chain, 0)
            link(dve.tensor_copy(firsts, bank[2][0:T, 0:E]))
            link(tt(ends, firsts, counts[:, :, P - 1], ALU.add))
            tt(counts, counts, firsts[:, :, None].broadcast_to([T, E, P]), ALU.add).then_inc(first_cp, 1)

            def hot_tile(e, u):
                ts(hot0[:, u, :], slot_row[:, :], firsts[:, e:e + 1] if isinstance(e, int) else
                   firsts[:, bass.ds(e, 1)], None, ALU.is_ge).then_inc(hot_half, 1)
                dve.wait_ge(hot_half, e + 1)
                dve.scalar_tensor_tensor(hot[:, u, :], slot_row[:, :], ends[:, e:e + 1] if isinstance(e, int) else
                                         ends[:, bass.ds(e, 1)], hot0[:, u, :], ALU.is_lt, ALU.mult)\
                   .then_inc(hot_ready, 1)

            def count_tokens(e, u):
                wait_past(dve, tok_cnt, e)
                dve.wait_ge(tok_ps, e + 1)
                for j in range(NHALF):
                    ins = ts(junk[:, j, :], bank[3 + u][:, j * P:(j + 1) * P], slot_col[:, j:j + 1], None, ALU.is_le,
                             ALU.add, accum_out=cnt[:, e, j:j + 1])
                ins.then_inc(tok_cnt, 1)

            hot_tile(0, 0)

            def two_experts(i):
                for u in range(2):
                    hot_tile(2 * i + u + 1, 1 - u)
                    count_tokens(2 * i + u, u)

            two_experts(0)
            with dve.Fori(1, E // 2 - 1) as i:
                two_experts(i)
            hot_tile(E - 1, 1)
            count_tokens(E - 2, 0)
            count_tokens(E - 1, 1)
            dve.wait_ge(tok_cnt, E)
            dve.wait_ge(tok_bv, E)
            trash = trash_col[:, None, :].broadcast_to([P, E, NHALF])
            link(tt(slot_tok, cnt, bv[:, :, :, 0], ALU.add))
            link(tt(slot_tok, slot_tok, trash, ALU.subtract))
            link(tt(slot_tok, slot_tok, bv[:, :, :, 1], ALU.mult))
            dve.tensor_copy(idx_all[:, E:E + 2, :], trash[:, 0:2, :])
            tt(idx_all[:, 0:E, :], slot_tok, trash, ALU.add).then_inc(idx_ready, 1)

            def is_first(c):
                return isinstance(c, int) and c == 0

            def decay_scans(c):
                dve.wait_ge(dec_in, 16 * (c + 1))
                for b in range(B):
                    dve.tensor_tensor_scan(Dt[:, b, :, :].rearrange("p h t -> p (h t)"), decay[:, b, :],
                                           eye_heads[:, :, :].rearrange("p h t -> p (h t)"), 0.0, ALU.mult,
                                           ALU.add).then_inc(scan_done, 1)
                dve.wait_ge(scan_done, 4 * (c + 1))

            def keys_weighted(c, h):
                dve.wait_ge(kt_ps, at(c, 8, h + 1))
                tt(kw[:, :, :], bank[3][:, :].rearrange("p (b d) -> p b d", b=B),
                   Dt[:, :, h, P - 1:P].broadcast_to([P, B, DK]), ALU.mult).then_inc(kw_cp, 1)

            def scores_decayed(c, h):
                dve.wait_ge(s_ps, at(c, 8, h + 1))
                tt(At[:, :, :], bank[2][:, :].rearrange("p (b t) -> p b t", b=B), Dt[:, :, h, :], ALU.mult)\
                    .then_inc(a_cp, 1)

            def head_out(c, h):
                part = t1[:, :, h * DV:(h + 1) * DV]
                inner = bank[5][:, 0:256].rearrange("p (b v) -> p b v", b=B)
                carried = bank[5][:, 256:512].rearrange("p (b v) -> p b v", b=B)
                added = bank[6][:, 0:256].rearrange("p (b v) -> p b v", b=B)
                dve.wait_ge(oi_ps, at(c, 8, h + 1))
                tt(part, carried, cum_all[:, c, :, h:h + 1].broadcast_to([P, B, DV]), ALU.mult)\
                    .then_inc(part_done, 1)
                if is_first(c):
                    dve.wait_ge(state_zero, 1)
                tt(state[:, h, :, :], state[:, h, :, :], last_all[:, c, :, h:h + 1].broadcast_to([P, B, DV]),
                   ALU.mult).then_inc(part_done, 1)
                dve.wait_ge(part_done, at(c, 16, 2 * h + 1))
                tt(part, part, inner, ALU.add).then_inc(oi_cp, 1)
                dve.wait_ge(part_done, at(c, 16, 2 * h + 2))
                dve.wait_ge(u_ps, at(c, 8, h + 1))
                tt(state[:, h, :, :], state[:, h, :, :], added, ALU.add).then_inc(state_up, 1)

            def gate(c, b):
                dve.wait_ge(og_cp, 4 * c + b + 1)
                dve.wait_ge(oi_cp, at(c, 8, 8))
                if not is_first(c):
                    dve.wait_ge(ot_ps, 4 * (c - 1) + b + 1)
                tt(gated[:, b, :], t1[:, b, :], og[:, b, :], ALU.mult).then_inc(gate_done, 1)

            def projected(c, b, final):
                dve.wait_ge(wo_ps, 4 * (c - 1) + b + 1)
                if not final:
                    dve.tensor_copy(kept[:, c - 1, b, :], bank[4][:, 0:D]).then_inc(wo_cp, 1)
                    return
                dve.wait_ge(accn_in, 16 * (c - E_STEPS))
                tt(res[:, b, :], bank[4][:, 0:D], acc_new[:, b, :], ALU.add).then_inc(wo_cp, 1)

            def finish_kept(c):
                dve.wait_ge(acco_in, 16 * (c - E_STEPS))
                tt(acc_old, acc_old, kept[:, c - 1 - E_STEPS, :, :], ALU.add).then_inc(old_ready, 1)

            def expert_hidden(c, j):
                e = (c - 1) * STEP_E + j
                dve.wait_ge(sg_ready, e + 1)
                tt(hs, bank[7][:, 0:CAP], sg, ALU.mult).then_inc(hs_ready, 1)
                dve.wait_ge(hs_ready, e + 1)
                tt(hT, hs, bank[7][:, CAP:2 * CAP], ALU.mult).then_inc(h_ready, 1)

            def expert_out(c, j):
                e = (c - 1) * STEP_E + j
                dve.wait_ge(y_ps, e + 1)
                dve.wait_ge(idx_cp, e + 2)
                for half in range(NHALF):
                    ins = ts(yb[:, j % 2, half, :], bank[7][:, half * D:(half + 1) * D],
                             xg[:, j % 2, half, bass.ds(D + e, 1)], None, ALU.mult)
                ins.then_inc(y_cp, 1)

            def step(c, experts, final):
                decay_scans(c)
                for s in range(1, H + 1):
                    keys_weighted(c, s - 1)
                    scores_decayed(c, s - 1)
                    if experts:
                        expert_hidden(c, s - 1)
                    if 4 <= s <= 7 and not is_first(c):
                        projected(c, s - 4, final)
                    head_out(c, s - 1)
                    if experts:
                        expert_out(c, s - 1)
                for b in range(B):
                    gate(c, b)
                if final:
                    finish_kept(c)

            step(0, False, False)
            with dve.Fori(1, E_STEPS + 1) as c:
                step(c, True, False)
            with dve.Fori(E_STEPS + 1, C) as c:
                step(c, False, True)
            for b in range(B):
                projected(C, b, True)
            finish_kept(C)


_INS = ["L0_attn_x", "L0_attn_Wq", "L0_attn_Wk", "L0_attn_Wv", "L0_attn_Wo", "L0_attn_Wg", "L0_attn_bg",
        "L0_attn_Wog", "L0_ffn_gate_w", "L0_ffn_gate_bias", "L0_ffn_w_gate", "L0_ffn_w_up", "L0_ffn_w_down"]
_OUTS = [((4, 2048, 256), "float32")]


def kernel(**inputs):
    import numpy as _np
    import concourse.bacc as _bacc
    from concourse import mybir as _mybir
    from concourse.bass_utils import run_bass_kernel_spmd as _run

    nc = _bacc.Bacc("TRN2", target_bir_lowering=False, num_devices=1)
    arrays, args = {}, []
    for name in _INS:
        a = _np.ascontiguousarray(inputs[name])
        arrays[f"in_{name}_dram"] = a
        args.append(nc.dram_tensor(f"in_{name}_dram", a.shape, _mybir.dt.from_np(a.dtype), kind="ExternalInput").ap())
    for i, (shape, dtype) in enumerate(_OUTS):
        dt = _mybir.dt.from_np(_np.dtype(dtype))
        args.append(nc.dram_tensor(f"out_{i}_dram", shape, dt, kind="ExternalOutput").ap())
    build(nc, *args)
    r = _run(nc, [arrays], core_ids=[0])
    return r.results[0]["out_0_dram"]
```

```python
from contextlib import ExitStack

import concourse.bass as bass
from concourse import mybir

F32 = mybir.dt.float32
BF16 = mybir.dt.bfloat16
F32R = mybir.dt.float32r
PARTS = ((0, 0), (0, 1), (1, 0))
U32 = mybir.dt.uint32
ALU = mybir.AluOpType
ACT = mybir.ActivationFunctionType
AX = mybir.AxisListType

P = 128
B, S, D = 4, 2048, 256
H, DK, DV = 8, 128, 64
HV = H * DV
KD = D // P
KO = HV // P
N = B * S
C = S // P
T = N // P
BP = B * P
E, I, G, TG, K = 64, 128, 8, 4, 8
EG = E // G
CAP = 256
NHALF = CAP // P
SCALE_OUT = 2.5
GATE_NORM = 16.0
NR = E + H
XW = D + E
ROWS = N + CAP
BIG = 3.0e38
TAKEN = 3.3e38
STEP_E = H
STEP_N = 3
S_COUNT = (C - 1) // STEP_N
S_SLOTS = S_COUNT + 1
E0 = S_SLOTS + 1
E1 = E0 + E // STEP_E
DIRECT = E0 - 1
ASIDE = E1 - 1 - DIRECT
N_CONSTS = 14
EB = 4
GROUPS_S = E // EB // H
SLOTS_S = E // H
NORM_CHAIN = 3
ROUTE_LINKS = (7, 5, 3, 5)
ROUTE_CHAIN = sum(ROUTE_LINKS)


def at(c, per, k):
    return c * per + k


def build(nc, x_in, Wq, Wk, Wv, Wo, Wg, bg, Wog, gate_w, gate_bias, w_gate, w_up, w_down, out):
    with ExitStack() as ctx:
        def sb(name, shape, dt=F32):
            return ctx.enter_context(nc.sbuf_tensor(name, shape, dt))

        def sem(name):
            return ctx.enter_context(nc.semaphore(name))

        xT_dram = nc.dram_tensor("xT_dram", (C, P, KD * BP), F32).ap()
        table = nc.dram_tensor("table", (ROWS, XW), F32).ap()
        decay_dram = nc.dram_tensor("decay_dram", (C, B * H, P), F32).ap()
        acc = nc.dram_tensor("acc", (ROWS, D), F32).ap()
        aside = nc.dram_tensor("aside", (ASIDE, P, B * D), F32).ap()

        bank = [ctx.enter_context(nc.psum_tensor(f"bank{i}", [P, 512], F32)) for i in range(8)]

        ident = sb("ident", [P, P])
        eye_heads = sb("eye_heads", [P, H, P])
        upper = sb("upper", [P, P], BF16)
        lower = sb("lower", [P, P], BF16)
        before = sb("before", [T, T], BF16)
        ones_t = sb("ones_t", [T, P], BF16)
        last_row = sb("last_row", [P, P])
        slot_row = sb("slot_row", [T, CAP], BF16)
        slot_col = sb("slot_col", [P, NHALF])
        trash_col = sb("trash_col", [P, NHALF])
        wq = sb("wq", [P, 2, KD, H * DK], F32R)
        wk = sb("wk", [P, 2, KD, H * DK], F32R)
        wv = sb("wv", [P, 2, KD, HV], F32R)
        wog = sb("wog", [P, 2, KD, HV], F32R)
        wo = sb("wo", [P, KO, D])

        cum_all = sb("cum_all", [P, C, B, H])
        last_all = sb("last_all", [P, C, B, H])
        sel_all = sb("sel_all", [P, E, B, C], BF16)
        idx_all = sb("idx_all", [P, E + 2, NHALF], U32)

        xs = sb("xs", [P, KD, BP])
        xp = sb("xp", [P, 2, KD, BP], F32R)
        decay = sb("decay", [P, B, H * P])
        Dt = sb("Dt", [P, B, H, P])
        qT = sb("qT", [P, 2, BP])
        kT = sb("kT", [P, 2, BP])
        kw = sb("kw", [P, B, DK])
        At = sb("At", [P, B, P])
        V = sb("V", [P, B, HV])
        og = sb("og", [P, B, HV])
        t1 = sb("t1", [P, B, HV])
        gated = sb("gated", [P, B, HV])
        addend = sb("addend", [P, B, D])
        res = sb("res", [P, B, D])
        oT = sb("oT", [P, HV])
        state = sb("state", [P, H, B, DV])

        ARENA = 6656
        arena = sb("arena", [P, ARENA])
        used = {}

        def view(phase, shape, dt=F32):
            words = 1
            for n in shape[1:]:
                words *= n
            lo = used.get(phase, 0)
            used[phase] = lo + words
            assert used[phase] <= ARENA, phase
            a = arena[0:shape[0], lo:lo + words]
            if dt is not F32:
                a = a.bitcast(dt)
            if len(shape) == 3:
                a = a.rearrange("p (a b) -> p a b", a=shape[1])
            if len(shape) == 4:
                a = a.rearrange("p (a b c) -> p a b c", a=shape[1], b=shape[2])
            return a

        raw = {}
        dt_flat = Dt[:, :, :, :].rearrange("p b h t -> p (b h t)")
        raw["q"] = dt_flat[:, 0:KD * H * DK].rearrange("p (k n) -> p k n", k=KD)
        raw["k"] = dt_flat[:, KD * H * DK:2 * KD * H * DK].rearrange("p (k n) -> p k n", k=KD)
        raw["v"] = qT[:, :, :]
        raw["og"] = kT[:, :, :]
        split_of = {"v": (wv, Wv), "q": (wq, Wq), "k": (wk, Wk), "og": (wog, Wog)}

        xt = view(1, [P, B, D])
        xn = view(1, [P, B, D])
        xnT = view(1, [P, KD, BP])
        wr = view(1, [P, KD, NR])
        gw_rows = view(1, [E, D])
        bias_e = view(1, [P, E])
        bias_g = view(1, [P, H])
        below = view(1, [P, G, G])
        above = view(1, [P, G, G])
        stats = view(1, [P, B, 6])
        mv = view(1, [P, B, 2])
        std = view(1, [P, B])
        rstd = view(1, [P, B])
        score = view(1, [P, B, E])
        zg = view(1, [P, B, H])
        alpha = view(1, [P, B, H])
        alphaT = view(1, [B * H, P])
        cumT = view(1, [B * H, P])
        zeros_t = view(1, [B * H, P])
        cum_c = view(1, [P, B * H])
        sfc = view(1, [P, B * G, EG])
        hi1 = view(1, [P, B * G, 4])
        lo1 = view(1, [P, B * G, 4])
        hi2 = view(1, [P, B * G, 2])
        lo2 = view(1, [P, B * G, 2])
        mid = view(1, [P, B * G, 2])
        hi3 = view(1, [P, B * G, 1])
        lo3 = view(1, [P, B * G, 1])
        gsc = view(1, [P, B, G])
        gt = view(1, [P, B * G, G])
        rank = view(1, [P, B * G])
        masked = view(1, [P, B, E])
        top8 = view(1, [P, B, K])
        left = gt.rearrange("p a b -> p (a b)").rearrange("p (b e) -> p b e", b=B)
        chosen = view(1, [P, B, E])
        total = view(1, [P, B])
        inv = view(1, [P, B])
        weight = view(1, [P, B, E])
        ge = view(1, [P, B * G, G])

        rise = view(2, [T, E * P // 2]).bitcast(BF16).rearrange("p (e t) -> p e t", e=E)
        totals = view(2, [T, E // 2]).bitcast(BF16)
        firsts = view(2, [T, E])
        reach = view(2, [T, 2, EB, CAP // 2])
        reach = reach.rearrange("p a b c -> p (a b c)").bitcast(BF16).rearrange("p (u e s) -> p u e s", u=2, e=EB)
        junk = view(2, [P, EB // 2 * NHALF, P])
        cnt = sb("cnt", [P, E, NHALF])
        tiles = sb("tiles", [P, E, NHALF])
        sums = sb("sums", [P, E])
        sel_cur = sb("sel_cur", [P, 2, EB, T + 1], BF16)

        idx = sb("idx", [P, 4, NHALF], U32)
        xg = view(3, [P, 2, NHALF, XW])
        xgT = view(3, [P, KD, CAP])
        wge = view(3, [P, 2, KD, I])
        wue = view(3, [P, 2, KD, I])
        wde = view(3, [P, 2, D])
        sg = view(3, [P, CAP])
        hs = view(3, [P, CAP])
        hT = view(3, [P, CAP])
        yb = view(3, [P, 2, NHALF, D])

        acc_old = view(4, [P, 2, B, D])
        att_old = view(4, [P, 2, B, D])

        x_tiles = x_in.rearrange("b (c p) d -> c p b d", p=P)
        out_tiles = out.rearrange("b (c p) d -> c p b d", p=P)
        acc_tiles = acc[0:N, :].rearrange("(b c p) d -> c p b d", b=B, c=C)
        acc_batch = acc[0:N, :].rearrange("(b s) d -> b s d", b=B)
        tab_tiles = table[0:N, :].rearrange("(b c p) w -> c p b w", b=B, c=C)

        w_in, w_const, w_ident, consts = sem("w_in"), sem("w_const"), sem("w_ident"), sem("consts")
        gwT_ps, gwT_cp = sem("gwT_ps"), sem("gwT_cp")
        init_acc, zero_rows = sem("init_acc"), sem("zero_rows")
        x_loaded = sem("x_loaded")
        mv_ready, std_ready, xn_ready = sem("mv_ready"), sem("std_ready"), sem("xn_ready")
        xn_stored, xT_stored, wt_stored, dec_stored = (sem("xn_stored"), sem("xT_stored"), sem("wt_stored"),
                                                       sem("dec_stored"))
        xT_ps, xT_cp, lg_ps = sem("xT_ps"), sem("xT_cp"), sem("lg_ps")
        score_ready, zg_ready, alpha_ready = sem("score_ready"), sem("zg_ready"), sem("alpha_ready")
        aT_ps, aT_cp, cumT_ready, cum_ps, cum_cp = (sem("aT_ps"), sem("aT_cp"), sem("cumT_ready"), sem("cum_ps"),
                                                    sem("cum_cp"))
        dec_ready, last_ps, last_cp = sem("dec_ready"), sem("last_ps"), sem("last_cp")
        weight_ready, sel_kept = sem("weight_ready"), sem("sel_kept")
        norm_chain, route_chain = sem("norm_chain"), sem("route_chain")
        selc_ready, cnt_ps, cnt_cp, first_ps, first_cp = (sem("selc_ready"), sem("cnt_ps"), sem("cnt_cp"),
                                                          sem("first_ps"), sem("first_cp"))
        tab_chain, reach_ready, tok_ps, tok_cnt, idx_ready = (sem("tab_chain"), sem("reach_ready"), sem("tok_ps"),
                                                              sem("tok_cnt"), sem("idx_ready"))
        xs_in, dec_in = sem("xs_in"), sem("dec_in")
        w_high, w_split, x_high, x_split = sem("w_high"), sem("w_split"), sem("x_high"), sem("x_split")
        qk_ps, qk_cp = sem("qk_ps"), sem("qk_cp")
        v_ps, v_cp, og_ps, og_cp = sem("v_ps"), sem("v_cp"), sem("og_ps"), sem("og_cp")
        kt_ps, kw_cp, s_ps, a_cp = sem("kt_ps"), sem("kw_cp"), sem("s_ps"), sem("a_cp")
        oi_ps, oi_cp, u_ps, state_up = sem("oi_ps"), sem("oi_cp"), sem("u_ps"), sem("state_up")
        ot_ps, ot_cp, wo_ps, wo_cp = sem("ot_ps"), sem("ot_cp"), sem("wo_ps"), sem("wo_cp")
        scan_done, part_done, gate_done = sem("scan_done"), sem("part_done"), sem("gate_done")
        state_zero = sem("state_zero")
        gathered = [sem("gathered0"), sem("gathered1")]
        ew_in = [sem("ew_in0"), sem("ew_in1")]
        idx_cp, scattered = sem("idx_cp"), sem("scattered")
        xg_ps, xg_cp, gu_ps, sg_ready, hs_ready, h_ready, y_ps, y_cp = (
            sem("xg_ps"), sem("xg_cp"), sem("gu_ps"), sem("sg_ready"), sem("hs_ready"), sem("h_ready"), sem("y_ps"),
            sem("y_cp"))
        add_in, res_out, direct_out = sem("add_in"), sem("res_out"), sem("direct_out")
        old_in, old_ready, old_out = [sem("old_in0"), sem("old_in1")], sem("old_ready"), sem("old_out")

        def wait_apart(eng, semaphore, value):
            if not isinstance(value, int):
                value = eng.snap(eng.to_reg(value))
            eng.wait_ge(consts, N_CONSTS)
            eng.wait_ge(semaphore, value)

        def wait_past(eng, semaphore, value):
            if not isinstance(value, int) or value > 0:
                eng.wait_ge(semaphore, value)

        block = ctx.enter_context(nc.Block())

        @block.sync
        def _(sp):
            sp.dma_start(gw_rows, gate_w).then_inc(w_const, 16)
            sp.dma_start(bias_e, gate_bias.rearrange("(a e) -> a e", a=1).broadcast_to([P, E])).then_inc(w_const, 16)
            sp.dma_start(bias_g, bg.rearrange("(a e) -> a e", a=1).broadcast_to([P, H])).then_inc(w_const, 16)
            sp.dma_start(wr[:, :, E:NR], Wg.rearrange("(k p) n -> p k n", k=KD)).then_inc(w_const, 16)
            def norm_io(c):
                wait_past(sp, xn_ready, c)
                sp.dma_start(xt, x_tiles[c]).then_inc(x_loaded, 16)
                sp.wait_ge(xn_ready, c + 1)
                sp.dma_start(tab_tiles[c][:, :, 0:D], xn).then_inc(xn_stored, 16)
                sp.wait_ge(xT_cp, 2 * (c + 1))
                sp.dma_start(xT_dram[c], xnT.rearrange("p k n -> p (k n)")).then_inc(xT_stored, 16)

            def load_xs(c):
                wait_apart(sp, xT_stored, 16 * (c + 1))
                wait_past(sp, x_split, c)
                sp.dma_start(xs[:, :, :].rearrange("p k n -> p (k n)"), xT_dram[c]).then_inc(xs_in, 16)

            def load_decay(c):
                wait_apart(sp, dec_stored, 16 * (c + 1))
                wait_past(sp, scan_done, 4 * c)
                src = decay_dram[c].rearrange("(a r) t -> a (r t)", a=1).broadcast_to([P, B * H * P])
                sp.dma_start(decay[:, :, :].rearrange("p b n -> p (b n)"), src).then_inc(dec_in, 16)

            def load_expert(e, slot):
                sp.dma_start(wge[:, slot], w_gate[e].rearrange("(k p) i -> p k i", k=KD)).then_inc(ew_in[slot], 16)
                sp.dma_start(wue[:, slot], w_up[e].rearrange("(k p) i -> p k i", k=KD)).then_inc(ew_in[slot], 16)
                sp.dma_start(wde[:, slot], w_down[e]).then_inc(ew_in[slot], 16)

            def load_addend(c, src):
                if not isinstance(c, int) or c > 1:
                    wait_apart(sp, wo_cp, 4 * (c - 1))
                    wait_apart(sp, res_out, 16 * (c - 1))
                sp.dma_start(addend[:, :, :], src).then_inc(add_in, 16)

            def store_res(c, dst):
                sp.wait_ge(wo_cp, 4 * c)
                sp.dma_start(dst, res[:, :, :]).then_inc(res_out, 16)

            def next_expert(c, j):
                e = (c - E0) * STEP_E + j
                sp.wait_ge(y_ps, e + 1)
                load_expert(e + 2, j % 2)

            def step(c, kind):
                first = isinstance(c, int) and c == 0
                if kind in ("norm", "lists") and not first:
                    load_addend(c, x_tiles[c - 1])
                if kind == "norm":
                    norm_io(STEP_N * c + 1)
                load_decay(c + 1)
                if kind == "norm":
                    norm_io(STEP_N * c + 2)
                    norm_io(STEP_N * c + 3)
                if kind == "experts":
                    for j in range(STEP_E - 1 if not isinstance(c, int) else STEP_E - 2):
                        next_expert(c, j)
                if kind in ("norm", "lists") and not first:
                    store_res(c, acc_tiles[c - 1])
                if kind == "experts":
                    wait_apart(sp, wo_cp, 4 * c)
                    sp.dma_start(aside[c - 1 - DIRECT].rearrange("p (b d) -> p b d", b=B), res[:, :, :])\
                      .then_inc(res_out, 16)
                load_xs(c + 1)
                if kind == "experts" and not isinstance(c, int):
                    next_expert(c, STEP_E - 1)

            for name in ("v", "q", "k", "og"):
                sp.dma_start(raw[name], split_of[name][1].rearrange("(k p) n -> p k n", k=KD)).then_inc(w_in, 16)
            sp.dma_start(wo[:, :, :], Wo.rearrange("(k p) n -> p k n", k=KO)).then_inc(w_in, 16)
            norm_io(0)
            load_xs(0)
            load_decay(0)
            step(0, "norm")
            for b in range(B):
                sp.dma_start(acc_batch[b][DIRECT * P:S, :], x_in[b][DIRECT * P:S, :]).then_inc(init_acc, 16)
            step(1, "norm")
            with sp.Fori(2, S_COUNT) as c:
                step(c, "norm")
            step(S_COUNT, "lists")
            step(S_SLOTS, "lists")
            sp.wait_ge(idx_ready, 1)
            load_expert(0, 0)
            load_expert(1, 1)
            with sp.Fori(E0, E1 - 1) as c:
                step(c, "experts")
            step(E1 - 1, "experts")

            sp.wait_ge(scattered, 16 * NHALF * E)
            for slot in range(2):
                sp.wait_ge(gathered[slot], 16 * NHALF * (E // 2 + 1))
            load_addend(C - 1, acc_tiles[C - 2])

            def load_old(i):
                sp.dma_start(acc_old[:, i % 2], acc_tiles[DIRECT + i]).then_inc(old_in[i % 2], 16)
                sp.dma_start(att_old[:, i % 2].rearrange("p b d -> p (b d)"), aside[i]).then_inc(old_in[i % 2], 16)

            load_old(0)
            load_old(1)
            for i in range(ASIDE):
                if i < DIRECT:
                    sp.dma_start(out_tiles[i], acc_tiles[i]).then_inc(direct_out, 16)
                sp.wait_ge(old_ready, i + 1)
                sp.dma_start(out_tiles[DIRECT + i], acc_old[:, i % 2]).then_inc(old_out, 16)
                if i + 2 < ASIDE:
                    sp.wait_ge(old_out, 16 * (i + 1))
                    load_old(i + 2)
            store_res(C - 1, out_tiles[C - 2])
            load_addend(C, acc_tiles[C - 1])
            store_res(C, out_tiles[C - 1])
            sp.wait_ge(direct_out, 16 * DIRECT)
            sp.wait_ge(old_out, 16 * ASIDE)
            sp.wait_ge(res_out, 16 * C)

        @block.gpsimd
        def _(pool):
            for m in (ident[:, :], last_row[:, :], upper[:, :], lower[:, :], before[:, :]):
                pool.memset(m, 1.0).then_inc(w_ident, 1)
            pool.memset(eye_heads[:, :, :], 1.0).then_inc(w_ident, 1)
            pool.memset(below, 1.0).then_inc(w_ident, 1)
            pool.memset(above, 1.0).then_inc(w_ident, 1)
            zeros = gated[:, 0, 0:XW]
            pool.memset(zeros, 0.0).then_inc(w_ident, 1)
            pool.wait_ge(w_ident, 9)
            pool.affine_select(out=ident[:, :], in_=ident[:, :], compare_op=ALU.is_equal, fill=0.0, base=0,
                               pattern=[[-1, P]], channel_multiplier=1).then_inc(consts, 1)
            pool.affine_select(out=last_row[:, :], in_=last_row[:, :], compare_op=ALU.is_equal, fill=0.0,
                               base=-(P - 1), pattern=[[0, P]], channel_multiplier=1).then_inc(consts, 1)
            pool.affine_select(out=upper[:, :], in_=upper[:, :], compare_op=ALU.is_ge, fill=0.0, base=0,
                               pattern=[[1, P]], channel_multiplier=-1).then_inc(consts, 1)
            pool.affine_select(out=lower[:, :], in_=lower[:, :], compare_op=ALU.is_gt, fill=0.0, base=0,
                               pattern=[[-1, P]], channel_multiplier=1).then_inc(consts, 1)
            pool.affine_select(out=before[:, :], in_=before[:, :], compare_op=ALU.is_gt, fill=0.0, base=0,
                               pattern=[[1, T]], channel_multiplier=-1).then_inc(consts, 1)
            pool.affine_select(out=eye_heads[:, :, :], in_=eye_heads[:, :, :], compare_op=ALU.is_equal, fill=0.0,
                               base=0, pattern=[[0, H], [-1, P]], channel_multiplier=1).then_inc(consts, 1)
            pool.affine_select(out=below, in_=below, compare_op=ALU.is_gt, fill=0.0, base=0,
                               pattern=[[1, G], [-1, G]], channel_multiplier=0).then_inc(consts, 1)
            pool.affine_select(out=above, in_=above, compare_op=ALU.is_gt, fill=0.0, base=0,
                               pattern=[[-1, G], [1, G]], channel_multiplier=0).then_inc(consts, 1)
            f = dict(allow_small_or_imprecise_dtypes=True)
            pool.iota(slot_row[:, :], [[1, CAP]], base=0, channel_multiplier=0, **f).then_inc(consts, 1)
            pool.iota(slot_col[:, :], [[P, NHALF]], base=0, channel_multiplier=1, **f).then_inc(consts, 1)
            pool.iota(trash_col[:, :], [[P, NHALF]], base=N, channel_multiplier=1, **f).then_inc(consts, 1)
            pool.memset(ones_t[:, :], 1.0).then_inc(consts, 1)
            pool.memset(sel_cur[:, :, :, 0:1], 0.0).then_inc(consts, 1)
            pool.memset(state[:, :, :, :], 0.0).then_inc(state_zero, 1)
            pool.memset(zeros_t, 0.0).then_inc(consts, 1)
            for j in range(NHALF):
                rows = slice(N + j * P, N + (j + 1) * P)
                pool.dma_start(table[rows, :], zeros).then_inc(zero_rows, 16)
                pool.dma_start(acc[rows, :], zeros[:, 0:D]).then_inc(zero_rows, 16)
            pool.wait_ge(zero_rows, 16 * 2 * NHALF)

            def routed(c):
                pool.wait_ge(dec_ready, c + 1)
                pool.dma_start(decay_dram[c], alphaT).then_inc(dec_stored, 16)
                pool.wait_ge(weight_ready, c + 1)
                pool.dma_start(tab_tiles[c][:, :, D:XW], weight).then_inc(wt_stored, 16)
                pool.tensor_copy(sel_all[:, :, :, c].rearrange("p e b -> p b e"), chosen).then_inc(sel_kept, 1)

            routed(0)
            with pool.Fori(1, C) as c:
                routed(c)

            def gather(e, u):
                pool.tensor_copy(idx[:, u % 4, :], idx_all[:, e, :]).then_inc(idx_cp, 1)
                wait_apart(pool, idx_cp, e + 1)
                for j in range(NHALF):
                    pool.indirect_dma_start(
                        out=xg[:, u % 2, j, :], out_offset=None, in_=table[:, :],
                        in_offset=bass.IndirectOffsetOnAxis(ap=idx[:, u % 4, j:j + 1], axis=0),
                        bounds_check=ROWS - 1, oob_is_err=True).then_inc(gathered[u % 2], 16)

            def scatter(e, u, j):
                if not isinstance(e, int) or e + j > 0:
                    wait_apart(pool, scattered, 16 * (NHALF * e + j))
                pool.indirect_dma_start(
                    out=acc[:, :], out_offset=bass.IndirectOffsetOnAxis(ap=idx[:, u % 4, j:j + 1], axis=0),
                    in_=yb[:, u % 2, j, :], in_offset=None, bounds_check=ROWS - 1, oob_is_err=True,
                    compute_op=ALU.add).then_inc(scattered, 16)

            pool.wait_ge(idx_ready, 1)
            pool.wait_ge(wt_stored, 16 * C)
            pool.wait_ge(xn_stored, 16 * C)
            gather(0, 0)
            gather(1, 1)
            pool.wait_ge(init_acc, 16 * B)
            def four_experts(i):
                for u in range(4):
                    e = 4 * i + u
                    pool.wait_ge(y_cp, e + 1)
                    scatter(e, u, 0)
                    gather(e + 2, u + 2)
                    scatter(e, u, 1)

            four_experts(0)
            with pool.Fori(1, E // 4) as i:
                four_experts(i)

            for i in range(ASIDE):
                pool.wait_ge(old_in[i % 2], 32 * (i // 2 + 1))
                pool.tensor_tensor(acc_old[:, i % 2], acc_old[:, i % 2], att_old[:, i % 2], ALU.add)\
                    .then_inc(old_ready, 1)

        @block.tensor
        def _(pe):
            mm, tr = pe.matmul, pe.transpose
            pe.wait_ge(consts, N_CONSTS)
            pe.wait_ge(w_const, 64)
            for k in range(KD):
                last = tr(bank[0][:, k * E:(k + 1) * E], gw_rows[:, k * P:(k + 1) * P], ident[0:E, 0:E])
            last.then_inc(gwT_ps, 1)
            pe.wait_ge(gwT_cp, 1)

            def tokens_back(c, k):
                if k == 0:
                    pe.wait_ge(xn_ready, c + 1)
                    wait_past(pe, last_cp, c)
                else:
                    pe.wait_ge(xT_cp, 2 * c + 1)
                for b in range(B):
                    last = tr(bank[7][:, b * P:(b + 1) * P], xn[:, b, k * P:(k + 1) * P], ident[:, :])
                last.then_inc(xT_ps, 1)

            def router(c):
                pe.wait_ge(xT_cp, 2 * (c + 1))
                for b in range(B):
                    for k in range(KD):
                        last = mm(bank[7][:, b * NR:(b + 1) * NR], xnT[:, k, b * P:(b + 1) * P], wr[:, k, :],
                                  start=(k == 0), stop=(k == KD - 1))
                last.then_inc(lg_ps, 1)

            def decays_across(c):
                pe.wait_ge(alpha_ready, c + 1)
                pe.wait_ge(score_ready, c + 1)
                tr(bank[7][0:B * H, 0:P], alpha.rearrange("p b h -> p (b h)"), ident[:, :]).then_inc(aT_ps, 1)

            def decays_back(c):
                wait_apart(pe, cumT_ready, c + 1)
                tr(bank[7][:, 0:B * H], cumT, ident[0:B * H, 0:B * H]).then_inc(cum_ps, 1)

            def decays_last(c):
                pe.wait_ge(cum_cp, c + 1)
                mm(bank[7][:, 0:B * H], last_row[:, :], cum_c, start=True, stop=True).then_inc(last_ps, 1)

            tokens_back(0, 0)
            tokens_back(0, 1)
            router(0)
            decays_across(0)
            decays_back(0)
            decays_last(0)

            def count_group(g):
                pe.wait_ge(selc_ready, g + 1)
                wait_past(pe, cnt_cp, g)
                if g == 0:
                    pe.wait_ge(last_cp, C)
                for j in range(EB):
                    dst = bank[7][0:T, j * P:(j + 1) * P]
                    mm(dst, sel_cur[:, g % 2, j, 1:T + 1], upper[:, :], start=True, stop=False)
                    last = mm(dst, sel_cur[:, g % 2, j, 0:T], lower[:, :], start=False, stop=True)
                last.then_inc(cnt_ps, 1)

            def first_counts():
                pe.wait_ge(cnt_cp, E // EB + 1)
                mm(bank[7][0:T, 0:E], before[:, :], totals, start=True, stop=True)
                mm(bank[7][:, E:2 * E], ones_t[:, :], totals, start=True, stop=True).then_inc(first_ps, 1)

            def slot_pair(n):
                pe.wait_ge(reach_ready, n // 2 + 1)
                wait_past(pe, tok_cnt, n)
                if n == 0:
                    pe.wait_ge(first_cp, 1)
                for j in range(2):
                    for half in range(NHALF):
                        lo = (j * NHALF + half) * P
                        last = mm(bank[7][:, lo:lo + P],
                                  reach[:, (n // 2) % 2, 2 * (n % 2) + j, half * P:(half + 1) * P],
                                  rise[:, 2 * n + j, :], start=True, stop=True)
                last.then_inc(tok_ps, 1)

            def proj_qk(c, h, which):
                u = 2 * h + which
                w = (wq, wk)[which]
                if not (isinstance(c, int) and at(c, 16, u) < 2):
                    pe.wait_ge(qk_cp, at(c, 16, u) - 1)
                for k in range(KD):
                    for i, (part, other) in enumerate(PARTS):
                        last = mm(bank[which][:, :], w[:, part, k, h * DK:(h + 1) * DK], xp[:, other, k, :],
                                  start=(k + i == 0), stop=(k == KD - 1 and i == 2))
                last.then_inc(qk_ps, 1)

            def bank4_free(c, item, b):
                first = isinstance(c, int) and c == 0
                if item == "v" and b == 0:
                    if not first:
                        pe.wait_ge(og_cp, 4 * c)
                        pe.wait_ge(oi_cp, 8 * (c - 1) + 7)
                elif item == "v":
                    pe.wait_ge(v_cp, 4 * c + b)
                elif item == "og" and b == 0:
                    pe.wait_ge(v_cp, 4 * c + 4)
                elif item == "og":
                    pe.wait_ge(og_cp, 4 * c + b)
                elif b == 0 and not (isinstance(c, int) and c == C):
                    pe.wait_ge(og_cp, 4 * c + 4)
                else:
                    pe.wait_ge(wo_cp, 4 * (c - 1) + b)

            def proj_tok(c, item, b):
                w, ready = {"v": (wv, v_ps), "og": (wog, og_ps)}[item]
                bank4_free(c, item, b)
                for k in range(KD):
                    for i, (part, other) in enumerate(PARTS):
                        last = mm(bank[4][:, :], xp[:, part, k, b * P:(b + 1) * P], w[:, other, k, :],
                                  start=(k + i == 0), stop=(k == KD - 1 and i == 2))
                last.then_inc(ready, 1)

            def keys_back(c, h):
                pe.wait_ge(qk_cp, at(c, 16, 2 * h + 2))
                if 5 <= h + 1 <= 8 and not (isinstance(c, int) and c == 0):
                    pe.wait_ge(ot_cp, 4 * (c - 1) + h - 3)
                elif not (isinstance(c, int) and c == 0 and h == 0):
                    pe.wait_ge(kw_cp, at(c, 8, h))
                for b in range(B):
                    last = tr(bank[3][:, b * P:(b + 1) * P], kT[:, h % 2, b * P:(b + 1) * P], ident[:, :])
                last.then_inc(kt_ps, 1)

            def scores(c, h):
                if not (isinstance(c, int) and c == 0 and h == 0):
                    pe.wait_ge(a_cp, at(c, 8, h))
                for b in range(B):
                    last = mm(bank[2][:, b * P:(b + 1) * P], kT[:, h % 2, b * P:(b + 1) * P],
                              qT[:, h % 2, b * P:(b + 1) * P], start=True, stop=True)
                last.then_inc(s_ps, 1)

            def outputs(c, h):
                pe.wait_ge(a_cp, at(c, 8, h + 1))
                pe.wait_ge(v_cp, 4 * c + 4)
                if not (isinstance(c, int) and c == 0 and h == 0):
                    pe.wait_ge(oi_cp, at(c, 8, h))
                for b in range(B):
                    mm(bank[5][:, b * DV:(b + 1) * DV], At[:, b, :], V[:, b, h * DV:(h + 1) * DV], start=True,
                       stop=True)
                if isinstance(c, int) and c == 0:
                    pe.wait_ge(state_zero, 1)
                else:
                    pe.wait_ge(state_up, at(c - 1, 8, h + 1))
                for b in range(B):
                    last = mm(bank[5][:, 256 + b * DV:256 + (b + 1) * DV], qT[:, h % 2, b * P:(b + 1) * P],
                              state[:, h, b, :], start=True, stop=True)
                last.then_inc(oi_ps, 1)

            def update(c, h):
                pe.wait_ge(kw_cp, at(c, 8, h + 1))
                if not (isinstance(c, int) and c == 0 and h == 0):
                    pe.wait_ge(state_up, at(c, 8, h))
                for b in range(B):
                    last = mm(bank[6][:, b * DV:(b + 1) * DV], kw[:, b, :], V[:, b, h * DV:(h + 1) * DV],
                              start=True, stop=True)
                last.then_inc(u_ps, 1)

            def outs_back(c, b):
                pe.wait_ge(gate_done, 4 * (c - 1) + b + 1)
                if isinstance(c, int) and c == C:
                    if b == 0:
                        pe.wait_ge(kw_cp, 8 * C)
                    else:
                        pe.wait_ge(ot_cp, 4 * (c - 1) + b)
                else:
                    pe.wait_ge(kw_cp, at(c, 8, b + 4))
                for j in range(KO):
                    last = tr(bank[3][:, j * P:(j + 1) * P], gated[:, b, j * P:(j + 1) * P], ident[:, :])
                last.then_inc(ot_ps, 1)

            def out_proj(c, b):
                bank4_free(c, "wo", b)
                pe.wait_ge(ot_cp, 4 * (c - 1) + b + 1)
                for j in range(KO):
                    last = mm(bank[4][:, 0:D], oT[:, j * P:(j + 1) * P], wo[:, j, :], start=(j == 0),
                              stop=(j == KO - 1))
                last.then_inc(wo_ps, 1)

            def expert_tokens(c, j):
                e = (c - E0) * STEP_E + j
                pe.wait_ge(gathered[j % 2], ((c - E0) * (STEP_E // 2) + j // 2 + 1) * 16 * NHALF)
                if j > 0:
                    pe.wait_ge(y_cp, e)
                else:
                    pe.wait_ge(gate_done, 4 * (c - 1) + 1)
                for k in range(KD):
                    for half in range(NHALF):
                        lo = k * CAP + half * P
                        last = tr(bank[7][:, lo:lo + P], xg[:, j % 2, half, k * P:(k + 1) * P], ident[:, :])
                last.then_inc(xg_ps, 1)

            def expert_hidden(c, j):
                e = (c - E0) * STEP_E + j
                pe.wait_ge(ew_in[j % 2], ((c - E0) * (STEP_E // 2) + j // 2 + 1) * 48)
                pe.wait_ge(xg_cp, e + 1)
                for m, w in enumerate((wge, wue)):
                    for k in range(KD):
                        last = mm(bank[7][:, m * CAP:(m + 1) * CAP], w[:, j % 2, k, :], xgT[:, k, :],
                                  start=(k == 0), stop=(k == KD - 1))
                last.then_inc(gu_ps, 1)

            def expert_down(c, j):
                e = (c - E0) * STEP_E + j
                pe.wait_ge(h_ready, e + 1)
                for half in range(NHALF):
                    last = mm(bank[7][:, half * D:(half + 1) * D], hT[:, half * P:(half + 1) * P],
                              wde[:, j % 2, :], start=True, stop=True)
                last.then_inc(y_ps, 1)

            def beside(c, kind, s, place):
                if kind == "norm":
                    n = STEP_N * c + 1 + s // 3
                    if s % 3 == 1:
                        (lambda: tokens_back(n, 0), lambda: tokens_back(n, 1), lambda: router(n), None)[place]() \
                            if place < 3 else None
                    if s % 3 == 2:
                        if place == 0:
                            decays_across(n)
                        if place == 2:
                            decays_back(n)
                        if place == 3:
                            decays_last(n)
                if kind == "count" and place in (0, 2) and s > 0:
                    count_group(GROUPS_S * (s - 1) + place // 2)
                if kind == "count" and place == 3 and s == H:
                    first_counts()
                if kind == "slots" and s > 0:
                    slot_pair(SLOTS_S // 2 * (s - 1) + place)
                if kind == "experts" and s > 0:
                    (expert_tokens, expert_hidden, None, expert_down)[place](c, s - 1) if place != 2 else None

            def step(c, kind):
                first = isinstance(c, int) and c == 0
                pe.wait_ge(x_split, c + 1)
                proj_tok(c, "v", 0)
                proj_qk(c, 0, 0)
                proj_tok(c, "v", 1)
                proj_qk(c, 0, 1)
                proj_tok(c, "v", 2)
                keys_back(c, 0)
                scores(c, 0)
                proj_tok(c, "v", 3)
                for s in range(1, H + 1):
                    if s > 1:
                        keys_back(c, s - 1)
                        scores(c, s - 1)
                    beside(c, kind, s, 0)
                    if s <= 4:
                        proj_tok(c, "og", s - 1)
                    if 4 <= s <= 7 and not first:
                        outs_back(c, s - 4)
                    if s < H:
                        proj_qk(c, s, 0)
                    beside(c, kind, s, 1)
                    if 4 <= s <= 7 and not first:
                        out_proj(c, s - 4)
                    if s < H:
                        proj_qk(c, s, 1)
                    beside(c, kind, s, 2)
                    outputs(c, s - 1)
                    update(c, s - 1)
                    beside(c, kind, s, 3)

            pe.wait_ge(w_in, 80)
            pe.wait_ge(w_split, 4)
            step(0, "norm")
            with pe.Fori(1, S_COUNT) as c:
                step(c, "norm")
            step(S_COUNT, "count")
            step(S_SLOTS, "slots")
            with pe.Fori(E0, E1) as c:
                step(c, "experts")
            step(C - 1, "last")
            for b in range(B):
                outs_back(C, b)
                out_proj(C, b)

        @block.scalar
        def _(act):
            f = nc.scalar.activation
            act.wait_ge(gwT_ps, 1)
            f(wr[:, :, 0:E], bank[0][:, 0:KD * E].rearrange("p (k e) -> p k e", k=KD), ACT.Copy).then_inc(gwT_cp, 1)

            def std_of(c):
                act.wait_ge(mv_ready, c + 1)
                f(std, mv[:, :, 1], ACT.Sqrt).then_inc(std_ready, 1)

            def sigmoids(c):
                act.wait_ge(zg_ready, c + 1)
                logits = bank[7][:, 0:B * NR].rearrange("p (b n) -> p b n", b=B)
                f(alpha, zg, ACT.Sigmoid, scale=1.0 / GATE_NORM).then_inc(alpha_ready, 1)
                wait_past(act, weight_ready, c)
                f(score, logits[:, :, 0:E], ACT.Sigmoid).then_inc(score_ready, 1)

            def tokens(c, k):
                act.wait_ge(xT_ps, 2 * c + k + 1)
                wait_past(act, xT_stored, 16 * c)
                f(xnT[:, k, :], bank[7][:, :], ACT.Copy).then_inc(xT_cp, 1)

            def tokens_high(c):
                act.wait_ge(xs_in, 16 * (c + 1))
                wait_past(act, qk_ps, 16 * c)
                wait_past(act, og_ps, 4 * c)
                f(xp[:, 0], xs[:, :, :], ACT.Copy).then_inc(x_high, 1)

            for i, (name, (w, _)) in enumerate(split_of.items()):
                act.wait_ge(w_in, 80)
                f(w[:, 0], raw[name], ACT.Copy).then_inc(w_high, 1)
            std_of(0)
            tokens(0, 0)
            tokens(0, 1)
            sigmoids(0)
            tokens_high(0)

            def select_group(g):
                if g == 0:
                    act.wait_ge(sel_kept, C)
                wait_past(act, cnt_ps, g - 1)
                act.copy(sel_cur[:, g % 2, :, 1:T + 1],
                         sel_all[:, g * EB:(g + 1) * EB, :, :].rearrange("p e b c -> p e (b c)"))\
                   .then_inc(selc_ready, 1)

            def qk_copy(c, h, which):
                act.wait_ge(qk_ps, at(c, 16, 2 * h + which + 1))
                dst, scale = ((qT, 1.0), (kT, float(DK) ** -0.5))[which]
                f(dst[:, h % 2, :], bank[which][:, :], ACT.Copy, scale=scale).then_inc(qk_cp, 1)

            def v_copy(c, b):
                act.wait_ge(v_ps, 4 * c + b + 1)
                f(V[:, b, :], bank[4][:, :], ACT.Copy).then_inc(v_cp, 1)

            def og_gate(c, b):
                act.wait_ge(og_ps, 4 * c + b + 1)
                if not (isinstance(c, int) and c == 0):
                    act.wait_ge(gate_done, 4 * (c - 1) + b + 1)
                f(og[:, b, :], bank[4][:, :], ACT.Sigmoid).then_inc(og_cp, 1)

            def outs_copy(c, b):
                act.wait_ge(ot_ps, 4 * (c - 1) + b + 1)
                f(oT[:, :], bank[3][:, :], ACT.Copy).then_inc(ot_cp, 1)

            def expert_tokens(c, j):
                e = (c - E0) * STEP_E + j
                act.wait_ge(xg_ps, e + 1)
                f(xgT.rearrange("p k n -> p (k n)"), bank[7][:, :], ACT.Copy).then_inc(xg_cp, 1)

            def expert_gate(c, j):
                e = (c - E0) * STEP_E + j
                act.wait_ge(gu_ps, e + 1)
                f(sg, bank[7][:, 0:CAP], ACT.Sigmoid).then_inc(sg_ready, 1)

            def beside(c, kind, s, place):
                if kind == "norm":
                    n = STEP_N * c + 1 + s // 3
                    if s % 3 == 0 and place == 1:
                        std_of(n)
                    if s % 3 == 1 and place == 0:
                        tokens(n, 0)
                    if s % 3 == 1 and place == 1:
                        tokens(n, 1)
                    if s % 3 == 1 and place == 2:
                        sigmoids(n)
                if kind == "count" and s > 0 and place in (0, 1):
                    select_group(GROUPS_S * (s - 1) + place)
                if kind == "experts" and s > 0 and place < 2:
                    (expert_tokens, expert_gate)[place](c, s - 1)

            def step(c, kind):
                first = isinstance(c, int) and c == 0
                v_copy(c, 0)
                qk_copy(c, 0, 0)
                v_copy(c, 1)
                qk_copy(c, 0, 1)
                v_copy(c, 2)
                v_copy(c, 3)
                beside(c, kind, 0, 1)
                for s in range(1, H + 1):
                    beside(c, kind, s, 0)
                    if s <= 4:
                        og_gate(c, s - 1)
                    if 4 <= s <= 7 and not first:
                        outs_copy(c, s - 4)
                    if s < H:
                        qk_copy(c, s, 0)
                    beside(c, kind, s, 1)
                    if s < H:
                        qk_copy(c, s, 1)
                    beside(c, kind, s, 2)
                    if s == H and kind != "last":
                        tokens_high(c + 1)

            step(0, "norm")
            with act.Fori(1, S_COUNT) as c:
                step(c, "norm")
            step(S_COUNT, "count")
            step(S_SLOTS, "slots")
            with act.Fori(E0, E1) as c:
                step(c, "experts")
            step(C - 1, "last")
            for b in range(B):
                outs_copy(C, b)

        @block.vector
        def _(dve):
            tt, ts = dve.tensor_tensor, dve.tensor_scalar

            def chained(semaphore, base):
                n = [0]

                def link(ins, apart=False):
                    n[0] += 1
                    ins.then_inc(semaphore, 1)
                    if apart:
                        wait_apart(dve, semaphore, base + n[0])
                    else:
                        dve.wait_ge(semaphore, base + n[0])
                return link, n

            dve.wait_ge(consts, N_CONSTS)
            dve.wait_ge(w_const, 64)

            def statistics(c):
                dve.wait_ge(x_loaded, 16 * (c + 1))
                link, n = chained(norm_chain, c * NORM_CHAIN)
                for b in range(B):
                    ins = dve.bn_stats(stats[:, b, :], xt[:, b, :])
                link(ins, apart=True)
                for b in range(B):
                    ins = dve.bn_aggr(mv[:, b, :], stats[:, b, :])
                link(ins)
                ts(mv[:, :, 1], mv[:, :, 1], 1e-5, None, ALU.add).then_inc(mv_ready, 1)

            def normalise(c):
                link, n = chained(norm_chain, c * NORM_CHAIN + 2)
                dve.wait_ge(std_ready, c + 1)
                link(dve.reciprocal(rstd, std))
                wait_past(dve, xn_stored, 16 * c)
                wait_past(dve, xT_ps, 2 * c)
                for b in range(B):
                    ins = ts(xn[:, b, :], xt[:, b, :], mv[:, b, 0:1], rstd[:, b:b + 1], ALU.subtract, ALU.mult)
                ins.then_inc(xn_ready, 1)

            def gates(c):
                dve.wait_ge(lg_ps, c + 1)
                logits = bank[7][:, 0:B * NR].rearrange("p (b n) -> p b n", b=B)
                tt(zg, logits[:, :, E:NR], bias_g[:, None, :].broadcast_to([P, B, H]), ALU.add).then_inc(zg_ready, 1)

            def decays_products(c):
                dve.wait_ge(aT_ps, c + 1)
                wait_past(dve, dec_stored, 16 * c)
                dve.tensor_copy(alphaT, bank[7][0:B * H, 0:P]).then_inc(aT_cp, 1)
                dve.wait_ge(aT_cp, c + 1)
                dve.tensor_tensor_scan(cumT, alphaT, zeros_t, 1.0, ALU.mult, ALU.add).then_inc(cumT_ready, 1)
                dve.wait_ge(cumT_ready, c + 1)
                dve.memset(alphaT[:, 0:1], 0.0).then_inc(dec_ready, 1)

            def decays_kept(c):
                dve.wait_ge(cum_ps, c + 1)
                dve.tensor_copy(cum_all[:, c, :, :].rearrange("p b h -> p (b h)"), bank[7][:, 0:B * H])
                dve.tensor_copy(cum_c, bank[7][:, 0:B * H]).then_inc(cum_cp, 1)

            def decays_last(c):
                dve.wait_ge(last_ps, c + 1)
                dve.tensor_copy(last_all[:, c, :, :].rearrange("p b h -> p (b h)"), bank[7][:, 0:B * H])\
                   .then_inc(last_cp, 1)

            def route_groups(c):
                link, n = chained(route_chain, c * ROUTE_CHAIN)
                dve.wait_ge(score_ready, c + 1)
                sfc_t = sfc.rearrange("p a b -> p (a b)").rearrange("p (b e) -> p b e", b=B)
                link(tt(sfc_t, score, bias_e[:, None, :].broadcast_to([P, B, E]), ALU.add))
                tt(hi1, sfc[:, :, 0:4], sfc[:, :, 4:8], ALU.max)
                link(tt(lo1, sfc[:, :, 0:4], sfc[:, :, 4:8], ALU.min))
                tt(mid, hi1[:, :, 0:2], hi1[:, :, 2:4], ALU.min)
                tt(hi2, hi1[:, :, 0:2], hi1[:, :, 2:4], ALU.max)
                link(tt(lo2, lo1[:, :, 0:2], lo1[:, :, 2:4], ALU.max))
                link(tt(lo2, lo2, mid, ALU.max))
                tt(mid[:, :, 0:1], hi2[:, :, 0:1], hi2[:, :, 1:2], ALU.min)
                tt(hi3, hi2[:, :, 0:1], hi2[:, :, 1:2], ALU.max)
                link(tt(lo3, lo2[:, :, 0:1], lo2[:, :, 1:2], ALU.max))
                link(tt(lo3, lo3, mid[:, :, 0:1], ALU.max))
                gsum = gsc.rearrange("p b g -> p (b g)")
                link(tt(gsum[:, :, None], hi3, lo3, ALU.add))
                assert n[0] == ROUTE_LINKS[0]

            def route_ranks(c):
                link, n = chained(route_chain, c * ROUTE_CHAIN + sum(ROUTE_LINKS[:1]))
                gt4 = gt.rearrange("p a b -> p (a b)").rearrange("p (b i j) -> p b i j", b=B, i=G)
                ge4 = ge.rearrange("p a b -> p (a b)").rearrange("p (b i j) -> p b i j", b=B, i=G)
                other = gsc[:, :, None, :].broadcast_to([P, B, G, G])
                own = gsc[:, :, :, None].broadcast_to([P, B, G, G])
                tt(gt4, other, own, ALU.is_gt)
                link(tt(ge4, other, own, ALU.is_ge))
                tt(gt4, gt4, above[:, None, :, :].broadcast_to([P, B, G, G]), ALU.mult)
                link(tt(ge4, ge4, below[:, None, :, :].broadcast_to([P, B, G, G]), ALU.mult))
                link(tt(gt4, gt4, ge4, ALU.add))
                link(dve.tensor_reduce(rank, gt, AX.X, ALU.add))
                link(ts(rank, rank, TG - 0.5, -BIG, ALU.is_ge, ALU.mult))
                assert n[0] == ROUTE_LINKS[1]

            def route_top(c):
                link, n = chained(route_chain, c * ROUTE_CHAIN + sum(ROUTE_LINKS[:2]))
                masked_g = masked.rearrange("p b e -> p (b e)").rearrange("p (a g) -> p a g", g=EG)
                ins = tt(masked_g, sfc, rank[:, :, None].broadcast_to([P, B * G, EG]), ALU.add)
                link(ins, apart=True)
                for b in range(B):
                    ins = dve.max(top8[:, b, :], masked[:, b, :])
                link(ins, apart=True)
                for b in range(B):
                    ins = dve.match_replace(left[:, b, :], top8[:, b, :], masked[:, b, :], -TAKEN)
                link(ins)
                assert n[0] == ROUTE_LINKS[2]

            def route_weights(c):
                link, n = chained(route_chain, c * ROUTE_CHAIN + sum(ROUTE_LINKS[:3]))
                wait_past(dve, sel_kept, c)
                wait_past(dve, wt_stored, 16 * c)
                link(tt(chosen, left, masked, ALU.not_equal))
                link(tt(weight, score, chosen, ALU.mult))
                link(dve.tensor_reduce(total, weight, AX.X, ALU.add))
                link(ts(total, total, 1e-20, None, ALU.add))
                link(dve.reciprocal(inv, total))
                dve.scalar_tensor_tensor(weight, weight, SCALE_OUT, inv[:, :, None].broadcast_to([P, B, E]),
                                         ALU.mult, ALU.mult).then_inc(weight_ready, 1)
                assert n[0] == ROUTE_LINKS[3]

            def tokens_low(c):
                dve.wait_ge(x_high, c + 1)
                tt(xp[:, 1], xs[:, :, :], xp[:, 0], ALU.subtract).then_inc(x_split, 1)

            for i, (name, (w, _)) in enumerate(split_of.items()):
                dve.wait_ge(w_high, i + 1)
                tt(w[:, 1], raw[name], w[:, 0], ALU.subtract).then_inc(w_split, 1)
            statistics(0)
            normalise(0)
            gates(0)
            decays_products(0)
            decays_kept(0)
            decays_last(0)

            tab_link, _ = chained(tab_chain, 0)

            def keep_group(g):
                dve.wait_ge(cnt_ps, g + 1)
                if g == 0:
                    for left_arena in (xn_stored, xT_stored, wt_stored, dec_stored):
                        dve.wait_ge(left_arena, 16 * C)
                dve.tensor_copy(rise[:, g * EB:(g + 1) * EB, :].rearrange("p e t -> p (e t)"), bank[7][0:T, :])\
                   .then_inc(cnt_cp, 1)

            def keep_totals():
                dve.wait_ge(cnt_cp, E // EB)
                dve.tensor_copy(totals, rise[:, :, P - 1]).then_inc(cnt_cp, 1)

            def keep_firsts():
                dve.wait_ge(first_ps, 1)
                tab_link(dve.memset(rise[:, :, P - 1:P], 1.0))
                dve.tensor_copy(sums[:, :], bank[7][:, E:2 * E])
                tab_link(dve.tensor_copy(firsts, bank[7][0:T, 0:E]))
                dve.nop().then_inc(first_cp, 1)

            def reach_group(g):
                wait_past(dve, tok_ps, 2 * (g - 1))
                for j in range(EB):
                    ins = ts(reach[:, g % 2, j, :], slot_row[:, :], firsts[:, EB * g + j:EB * g + j + 1], None,
                             ALU.is_ge)
                ins.then_inc(reach_ready, 1)

            def count_pair(n):
                wait_past(dve, tok_cnt, n)
                dve.wait_ge(tok_ps, n + 1)
                for j in range(2 * NHALF):
                    half = j % NHALF
                    ts(junk[:, j, 0:P - 1], bank[7][:, j * P:j * P + P - 1], slot_col[:, half:half + 1], None,
                       ALU.is_le, ALU.add, accum_out=cnt[:, 2 * n + j // NHALF, half:half + 1])
                last_cols = bank[7][:, :].rearrange("p (e h t) -> p e h t", e=2, h=NHALF)[:, :, :, P - 1]
                dve.tensor_copy(tiles[:, 2 * n:2 * n + 2, :], last_cols).then_inc(tok_cnt, 1)

            def make_lists():
                dve.wait_ge(tok_cnt, E // 2)
                trash = trash_col[:, None, :].broadcast_to([P, E, NHALF])
                slots = slot_col[:, None, :].broadcast_to([P, E, NHALF])
                tab_link(dve.scalar_tensor_tensor(cnt[:, :, :], tiles[:, :, :], float(P), cnt[:, :, :], ALU.mult,
                                                  ALU.add))
                tab_link(dve.scalar_tensor_tensor(cnt[:, :, :], cnt[:, :, :], -float(P), trash, ALU.add,
                                                  ALU.subtract))
                tab_link(tt(tiles[:, :, :], sums[:, :, None].broadcast_to([P, E, NHALF]), slots, ALU.is_gt))
                tab_link(tt(cnt[:, :, :], cnt[:, :, :], tiles[:, :, :], ALU.mult))
                dve.tensor_copy(idx_all[:, E:E + 2, :], trash[:, 0:2, :])
                tt(idx_all[:, 0:E, :], cnt[:, :, :], trash, ALU.add).then_inc(idx_ready, 1)

            def is_first(c):
                return isinstance(c, int) and c == 0

            def decay_scans(c):
                dve.wait_ge(dec_in, 16 * (c + 1))
                for b in range(B):
                    dve.tensor_tensor_scan(Dt[:, b, :, :].rearrange("p h t -> p (h t)"), decay[:, b, :],
                                           eye_heads[:, :, :].rearrange("p h t -> p (h t)"), 0.0, ALU.mult,
                                           ALU.add).then_inc(scan_done, 1)
                dve.wait_ge(scan_done, 4 * (c + 1))

            def keys_weighted(c, h):
                dve.wait_ge(kt_ps, at(c, 8, h + 1))
                tt(kw[:, :, :], bank[3][:, :].rearrange("p (b d) -> p b d", b=B),
                   Dt[:, :, h, P - 1:P].broadcast_to([P, B, DK]), ALU.mult).then_inc(kw_cp, 1)

            def scores_decayed(c, h):
                dve.wait_ge(s_ps, at(c, 8, h + 1))
                tt(At[:, :, :], bank[2][:, :].rearrange("p (b t) -> p b t", b=B), Dt[:, :, h, :], ALU.mult)\
                    .then_inc(a_cp, 1)

            def head_out(c, h):
                part = t1[:, :, h * DV:(h + 1) * DV]
                inner = bank[5][:, 0:256].rearrange("p (b v) -> p b v", b=B)
                carried = bank[5][:, 256:512].rearrange("p (b v) -> p b v", b=B)
                added = bank[6][:, 0:256].rearrange("p (b v) -> p b v", b=B)
                dve.wait_ge(oi_ps, at(c, 8, h + 1))
                tt(part, carried, cum_all[:, c, :, h:h + 1].broadcast_to([P, B, DV]), ALU.mult)\
                    .then_inc(part_done, 1)
                if is_first(c):
                    dve.wait_ge(state_zero, 1)
                tt(state[:, h, :, :], state[:, h, :, :], last_all[:, c, :, h:h + 1].broadcast_to([P, B, DV]),
                   ALU.mult).then_inc(part_done, 1)
                dve.wait_ge(part_done, at(c, 16, 2 * h + 1))
                tt(part, part, inner, ALU.add).then_inc(oi_cp, 1)
                dve.wait_ge(part_done, at(c, 16, 2 * h + 2))
                dve.wait_ge(u_ps, at(c, 8, h + 1))
                tt(state[:, h, :, :], state[:, h, :, :], added, ALU.add).then_inc(state_up, 1)

            def gate(c, b):
                dve.wait_ge(og_cp, 4 * c + b + 1)
                dve.wait_ge(oi_cp, at(c, 8, 8))
                if not is_first(c):
                    dve.wait_ge(ot_ps, 4 * (c - 1) + b + 1)
                tt(gated[:, b, :], t1[:, b, :], og[:, b, :], ALU.mult).then_inc(gate_done, 1)

            def projected(c, b, kind):
                dve.wait_ge(wo_ps, 4 * (c - 1) + b + 1)
                if kind == "experts":
                    if b == 0:
                        dve.wait_ge(res_out, 16 * (c - 1))
                    dve.tensor_copy(res[:, b, :], bank[4][:, 0:D]).then_inc(wo_cp, 1)
                    return
                dve.wait_ge(add_in, 16 * (c if kind not in ("last", "end") else c - ASIDE))
                tt(res[:, b, :], bank[4][:, 0:D], addend[:, b, :], ALU.add).then_inc(wo_cp, 1)

            def expert_hidden(c, j):
                e = (c - E0) * STEP_E + j
                dve.wait_ge(sg_ready, e + 1)
                tt(hs, bank[7][:, 0:CAP], sg, ALU.mult).then_inc(hs_ready, 1)
                dve.wait_ge(hs_ready, e + 1)
                tt(hT, hs, bank[7][:, CAP:2 * CAP], ALU.mult).then_inc(h_ready, 1)

            def expert_out(c, j):
                e = (c - E0) * STEP_E + j
                dve.wait_ge(y_ps, e + 1)
                dve.wait_ge(idx_cp, e + 2)
                for half in range(NHALF):
                    ins = ts(yb[:, j % 2, half, :], bank[7][:, half * D:(half + 1) * D],
                             xg[:, j % 2, half, bass.ds(D + e, 1)], None, ALU.mult)
                ins.then_inc(y_cp, 1)

            def beside(c, kind, s, place):
                if kind == "norm":
                    n = STEP_N * c + 1 + s // 3
                    if s % 3 == 0:
                        if place == 0:
                            statistics(n)
                        if place == 3:
                            normalise(n)
                        if place == (1 if s > 0 else 3):
                            route_ranks(n - 1)
                    if s % 3 == 1 and place < 3:
                        (route_top, route_weights, None)[place](n - 1) if place < 2 else gates(n)
                    if s % 3 == 2:
                        (decays_products, route_groups, decays_kept, decays_last)[place](n)
                if kind == "count" and s == 0 and place == 3:
                    for part in (route_ranks, route_top, route_weights):
                        part(C - 1)
                if kind == "count" and s > 0:
                    if place in (1, 3):
                        keep_group(GROUPS_S * (s - 1) + place // 2)
                    if place == 3 and s == H:
                        keep_totals()
                if kind == "slots" and s == 0 and place == 3:
                    keep_firsts()
                    reach_group(0)
                if kind == "slots" and s > 0:
                    n = SLOTS_S // 2 * (s - 1) + place
                    if n % 2 == 0 and n // 2 + 1 < E // EB:
                        reach_group(n // 2 + 1)
                    count_pair(n)
                    if n == E // 2 - 1:
                        make_lists()
                if kind == "experts" and s > 0:
                    if place == 1:
                        expert_hidden(c, s - 1)
                    if place == 3:
                        expert_out(c, s - 1)

            def step(c, kind):
                beside(c, kind, 0, 0)
                decay_scans(c)
                beside(c, kind, 0, 3)
                for s in range(1, H + 1):
                    keys_weighted(c, s - 1)
                    scores_decayed(c, s - 1)
                    beside(c, kind, s, 0)
                    beside(c, kind, s, 1)
                    if 4 <= s <= 7 and not is_first(c):
                        projected(c, s - 4, kind)
                    beside(c, kind, s, 2)
                    head_out(c, s - 1)
                    beside(c, kind, s, 3)
                if kind != "last":
                    tokens_low(c + 1)
                for b in range(B):
                    gate(c, b)

            route_groups(0)
            tokens_low(0)
            step(0, "norm")
            with dve.Fori(1, S_COUNT) as c:
                step(c, "norm")
            step(S_COUNT, "count")
            step(S_SLOTS, "slots")
            with dve.Fori(E0, E1) as c:
                step(c, "experts")
            step(C - 1, "last")
            for b in range(B):
                projected(C, b, "end")


_INS = ["L0_attn_x", "L0_attn_Wq", "L0_attn_Wk", "L0_attn_Wv", "L0_attn_Wo", "L0_attn_Wg", "L0_attn_bg",
        "L0_attn_Wog", "L0_ffn_gate_w", "L0_ffn_gate_bias", "L0_ffn_w_gate", "L0_ffn_w_up", "L0_ffn_w_down"]
_OUTS = [((4, 2048, 256), "float32")]


def kernel(**inputs):
    import numpy as _np
    import concourse.bacc as _bacc
    from concourse import mybir as _mybir
    from concourse.bass_utils import run_bass_kernel_spmd as _run

    nc = _bacc.Bacc("TRN2", target_bir_lowering=False, num_devices=1)
    arrays, args = {}, []
    for name in _INS:
        a = _np.ascontiguousarray(inputs[name])
        arrays[f"in_{name}_dram"] = a
        args.append(nc.dram_tensor(f"in_{name}_dram", a.shape, _mybir.dt.from_np(a.dtype), kind="ExternalInput").ap())
    for i, (shape, dtype) in enumerate(_OUTS):
        dt = _mybir.dt.from_np(_np.dtype(dtype))
        args.append(nc.dram_tensor(f"out_{i}_dram", shape, dt, kind="ExternalOutput").ap())
    build(nc, *args)
    r = _run(nc, [arrays], core_ids=[0])
    return r.results[0]["out_0_dram"]
```

```python
from contextlib import ExitStack

import concourse.bass as bass
from concourse import mybir

F32 = mybir.dt.float32
BF16 = mybir.dt.bfloat16
F32R = mybir.dt.float32r
PARTS = ((0, 0), (0, 1), (1, 0))
U32 = mybir.dt.uint32
ALU = mybir.AluOpType
ACT = mybir.ActivationFunctionType
AX = mybir.AxisListType

P = 128
B, S, D = 4, 2048, 256
H, DK, DV = 8, 128, 64
HV = H * DV
KD = D // P
KO = HV // P
N = B * S
C = S // P
T = N // P
BP = B * P
E, I, G, TG, K = 64, 128, 8, 4, 8
EG = E // G
CAP = 256
NHALF = CAP // P
SCALE_OUT = 2.5
GATE_NORM = 16.0
NR = E + H
XW = D + E
ROWS = N + CAP
BIG = 3.0e38
TAKEN = 3.3e38
STEP_E = H
STEP_N = 3
S_COUNT = (C - 1) // STEP_N
S_SLOTS = S_COUNT + 1
E0 = S_SLOTS + 1
E1 = E0 + E // STEP_E
DIRECT = E0 - 1
ASIDE = E1 - 1 - DIRECT
N_CONSTS = 13
EB = 4
COUNT_AT = [(s, place) for s in range(2, H + 1) for place in ((1, 2, 3) if s < 4 else (1, 3))]
assert len(COUNT_AT) == E // EB
SLOTS_S = E // H
NORM_CHAIN = 3
ROUTE_LINKS = (7, 5, 3, 5)
ROUTE_CHAIN = sum(ROUTE_LINKS)


def at(c, per, k):
    return c * per + k


def build(nc, x_in, Wq, Wk, Wv, Wo, Wg, bg, Wog, gate_w, gate_bias, w_gate, w_up, w_down, out):
    with ExitStack() as ctx:
        def sb(name, shape, dt=F32):
            return ctx.enter_context(nc.sbuf_tensor(name, shape, dt))

        def sem(name):
            return ctx.enter_context(nc.semaphore(name))

        xT_dram = nc.dram_tensor("xT_dram", (C, P, KD * BP), F32).ap()
        table = nc.dram_tensor("table", (ROWS, XW), F32).ap()
        decay_dram = nc.dram_tensor("decay_dram", (C, B * H, P), F32).ap()
        acc = nc.dram_tensor("acc", (ROWS, D), F32).ap()
        aside = nc.dram_tensor("aside", (ASIDE, P, B * D), F32).ap()

        bank = [ctx.enter_context(nc.psum_tensor(f"bank{i}", [P, 512], F32)) for i in range(8)]

        ident = sb("ident", [P, P])
        eye_heads = sb("eye_heads", [P, H, P])
        upper = sb("upper", [P, P], BF16)
        lower = sb("lower", [P, P], BF16)
        before = sb("before", [T, T], BF16)
        ones_t = sb("ones_t", [T, P], BF16)
        last_row = sb("last_row", [P, P])
        slot_col = sb("slot_col", [P, NHALF])
        trash_col = sb("trash_col", [P, NHALF])
        wq = sb("wq", [P, 2, KD, H * DK], F32R)
        wk = sb("wk", [P, 2, KD, H * DK], F32R)
        wv = sb("wv", [P, 2, KD, HV], F32R)
        wog = sb("wog", [P, 2, KD, HV], F32R)
        wo = sb("wo", [P, 2, KO, D], F32R)

        cum_all = sb("cum_all", [P, C, B, H])
        last_all = sb("last_all", [P, C, B, H])
        sel_all = sb("sel_all", [P, E, B, C], BF16)
        idx_all = sb("idx_all", [P, E + 2, NHALF], U32)

        xs = sb("xs", [P, KD, BP])
        xp = sb("xp", [P, 2, KD, BP], F32R)
        decay = sb("decay", [P, B, H * P])
        Dt = sb("Dt", [P, B, H, P])
        qT = sb("qT", [P, 2, BP])
        kT = sb("kT", [P, 2, BP])
        kw = sb("kw", [P, B, DK])
        At = sb("At", [P, B, P])
        V = sb("V", [P, B, HV])
        og = sb("og", [P, B, HV])
        t1 = sb("t1", [P, B, HV])
        gated = sb("gated", [P, B, HV])
        addend = sb("addend", [P, B, D])
        res = sb("res", [P, B, D])
        oT = sb("oT", [P, 2, HV], F32R)
        state = sb("state", [P, H, B, DV])

        ARENA = 5120
        arena = sb("arena", [P, ARENA])
        used = {}

        def view(phase, shape, dt=F32):
            words = 1
            for n in shape[1:]:
                words *= n
            lo = used.get(phase, 0)
            used[phase] = lo + words
            assert used[phase] <= ARENA, phase
            a = arena[0:shape[0], lo:lo + words]
            if dt is not F32:
                a = a.bitcast(dt)
            if len(shape) == 3:
                a = a.rearrange("p (a b) -> p a b", a=shape[1])
            if len(shape) == 4:
                a = a.rearrange("p (a b c) -> p a b c", a=shape[1], b=shape[2])
            return a

        raw = {}
        dt_flat = Dt[:, :, :, :].rearrange("p b h t -> p (b h t)")
        raw["q"] = dt_flat[:, 0:KD * H * DK].rearrange("p (k n) -> p k n", k=KD)
        raw["k"] = dt_flat[:, KD * H * DK:2 * KD * H * DK].rearrange("p (k n) -> p k n", k=KD)
        raw["v"] = qT[:, :, :]
        raw["og"] = kT[:, :, :]
        raw["o"] = og[:, 0:2, :].rearrange("p b n -> p (b n)").rearrange("p (k n) -> p k n", k=KO)
        split_of = {"v": (wv, Wv), "q": (wq, Wq), "k": (wk, Wk), "og": (wog, Wog), "o": (wo, Wo)}

        xt = view(1, [P, B, D])
        xn = xt
        xnT = view(1, [P, KD, BP])
        wr = view(1, [P, KD, NR])
        bias_e = view(1, [P, E])
        bias_g = view(1, [P, H])
        below = view(1, [P, G, G])
        above = view(1, [P, G, G])
        stats = view(1, [P, B, 6])
        mv = view(1, [P, B, 2])
        std = view(1, [P, B])
        rstd = view(1, [P, B])
        score = view(1, [P, B, E])
        zg = view(1, [P, B, H])
        alpha = view(1, [P, B, H])
        alphaT = view(1, [B * H, P])
        cumT = view(1, [B * H, P])
        zeros_t = view(1, [B * H, P])
        cum_c = view(1, [P, B * H])
        sfc = view(1, [P, B * G, EG])
        ge = view(1, [P, B * G, G])
        pairs = ge.rearrange("p a b -> p (a b)").rearrange("p (u a b) -> p u a b", u=2, a=B * G)
        hi1, lo1 = pairs[:, 0], pairs[:, 1]
        hi2 = view(1, [P, B * G, 2])
        lo2 = view(1, [P, B * G, 2])
        mid = view(1, [P, B * G, 2])
        hi3 = view(1, [P, B * G, 1])
        lo3 = view(1, [P, B * G, 1])
        gsc = view(1, [P, B, G])
        gt = view(1, [P, B * G, G])
        rank = view(1, [P, B * G])
        masked = view(1, [P, B, E])
        gw_rows = masked[0:E, :, :].rearrange("p b e -> p (b e)")
        top8 = view(1, [P, B, K])
        left = gt.rearrange("p a b -> p (a b)").rearrange("p (b e) -> p b e", b=B)
        chosen = view(1, [P, B, E])
        total = view(1, [P, B])
        inv = view(1, [P, B])
        weight = view(1, [P, B, E])

        rise = view(2, [T, E * P // 2]).bitcast(BF16).rearrange("p (e t) -> p e t", e=E)
        slot_row = view(2, [T, CAP // 2]).bitcast(BF16)
        totals = view(2, [T, E // 2]).bitcast(BF16)
        firsts = view(2, [T, E])
        reach = sel_all[0:T, :, :, :].rearrange("p e b c -> p (e b c)")[:, 0:2 * EB * CAP]
        reach = reach.rearrange("p (u e s) -> p u e s", u=2, e=EB)
        junk = view(2, [P, EB // 2 * NHALF, P])
        cnt = view(2, [P, E, NHALF])
        tiles = view(2, [P, E, NHALF])
        sums = sb("sums", [P, E])
        sel_cur = sb("sel_cur", [P, 2, EB, T + 1], BF16)

        idx = sb("idx", [P, 4, NHALF], U32)
        xg = view(3, [P, 2, NHALF, XW])
        xgT = oT
        wgu = view(3, [P, 2, 2, KD * I])
        wgu_p = sb("wgu_p", [P, 2, 2, KD * I], F32R)
        wde = view(3, [P, 2, D])
        sg = view(3, [P, CAP])
        hT = sg
        yb = view(3, [P, 2, NHALF, D])

        acc_old = view(4, [P, 2, B, D])
        att_old = view(4, [P, 2, B, D])

        addend_end = xs[:, :, :].rearrange("p k n -> p (k n)").rearrange("p (b d) -> p b d", b=B)
        res_end = qT[:, :, :].rearrange("p u n -> p (u n)").rearrange("p (b d) -> p b d", b=B)
        oT_end = xp[:, 0:2, 0, :]

        def back_at(c, b):
            if isinstance(c, int) and c == C and b % 2:
                return bank[2], oT_end, bank[5]
            return bank[3], oT[:, :, :], bank[4]

        x_tiles = x_in.rearrange("b (c p) d -> c p b d", p=P)
        out_tiles = out.rearrange("b (c p) d -> c p b d", p=P)
        acc_tiles = acc[0:N, :].rearrange("(b c p) d -> c p b d", b=B, c=C)
        acc_batch = acc[0:N, :].rearrange("(b s) d -> b s d", b=B)
        tab_tiles = table[0:N, :].rearrange("(b c p) w -> c p b w", b=B, c=C)

        w_in, w_const, w_ident, consts = sem("w_in"), sem("w_const"), sem("w_ident"), sem("consts")
        gwT_ps, gwT_cp = sem("gwT_ps"), sem("gwT_cp")
        init_acc, zero_rows = sem("init_acc"), sem("zero_rows")
        x_loaded = sem("x_loaded")
        mv_ready, std_ready, xn_ready = sem("mv_ready"), sem("std_ready"), sem("xn_ready")
        xn_stored, xT_stored, wt_stored, dec_stored = (sem("xn_stored"), sem("xT_stored"), sem("wt_stored"),
                                                       sem("dec_stored"))
        xT_ps, xT_cp, lg_ps = sem("xT_ps"), sem("xT_cp"), sem("lg_ps")
        score_ready, zg_ready, alpha_ready = sem("score_ready"), sem("zg_ready"), sem("alpha_ready")
        aT_ps, aT_cp, cumT_ready, cum_ps, cum_cp = (sem("aT_ps"), sem("aT_cp"), sem("cumT_ready"), sem("cum_ps"),
                                                    sem("cum_cp"))
        dec_ready, last_ps, last_cp = sem("dec_ready"), sem("last_ps"), sem("last_cp")
        weight_ready, sel_kept = sem("weight_ready"), sem("sel_kept")
        norm_chain, route_chain = sem("norm_chain"), sem("route_chain")
        selc_ready, cnt_ps, cnt_cp, first_ps, first_cp = (sem("selc_ready"), sem("cnt_ps"), sem("cnt_cp"),
                                                          sem("first_ps"), sem("first_cp"))
        slot_row_ready = sem("slot_row_ready")
        tab_chain, reach_ready, tok_ps, tok_cnt, idx_ready = (sem("tab_chain"), sem("reach_ready"), sem("tok_ps"),
                                                              sem("tok_cnt"), sem("idx_ready"))
        xs_in, dec_in = sem("xs_in"), sem("dec_in")
        w_high, w_split, x_high, x_split = sem("w_high"), sem("w_split"), sem("x_high"), sem("x_split")
        w_split_pool = sem("w_split_pool")
        qk_ps, qk_cp = sem("qk_ps"), sem("qk_cp")
        v_ps, v_cp, og_ps, og_cp = sem("v_ps"), sem("v_cp"), sem("og_ps"), sem("og_cp")
        kt_ps, kw_cp, s_ps, a_cp = sem("kt_ps"), sem("kw_cp"), sem("s_ps"), sem("a_cp")
        oi_ps, oi_cp, u_ps, state_up = sem("oi_ps"), sem("oi_cp"), sem("u_ps"), sem("state_up")
        ot_high = sem("ot_high")
        ot_ps, ot_cp, wo_ps, wo_cp = sem("ot_ps"), sem("ot_cp"), sem("wo_ps"), sem("wo_cp")
        scan_done, part_done, gate_done = sem("scan_done"), sem("part_done"), sem("gate_done")
        gathered = [sem("gathered0"), sem("gathered1")]
        ew_in = [sem("ew_in0"), sem("ew_in1")]
        idx_cp, scattered = sem("idx_cp"), sem("scattered")
        wgu_high, wgu_split, xg_high = sem("wgu_high"), sem("wgu_split"), sem("xg_high")
        xg_ps, xg_cp, gu_ps, sg_ready, hs_ready, h_ready, y_ps, y_cp = (
            sem("xg_ps"), sem("xg_cp"), sem("gu_ps"), sem("sg_ready"), sem("hs_ready"), sem("h_ready"), sem("y_ps"),
            sem("y_cp"))
        add_in, res_out, direct_out = sem("add_in"), sem("res_out"), sem("direct_out")
        old_in, old_ready, old_out = [sem("old_in0"), sem("old_in1")], sem("old_ready"), sem("old_out")

        def wait_apart(eng, semaphore, value):
            if not isinstance(value, int):
                value = eng.snap(eng.to_reg(value))
            eng.wait_ge(consts, N_CONSTS)
            eng.wait_ge(semaphore, value)

        def is_first(c):
            return isinstance(c, int) and c == 0

        def is_last(c):
            return isinstance(c, int) and c == C - 1

        def wait_past(eng, semaphore, value):
            if not isinstance(value, int) or value > 0:
                eng.wait_ge(semaphore, value)

        block = ctx.enter_context(nc.Block())

        @block.sync
        def _(sp):
            sp.dma_start(xt, x_tiles[0]).then_inc(x_loaded, 16)
            sp.dma_start(gw_rows, gate_w).then_inc(w_const, 16)
            sp.dma_start(bias_e, gate_bias.rearrange("(a e) -> a e", a=1).broadcast_to([P, E])).then_inc(w_const, 16)
            sp.dma_start(bias_g, bg.rearrange("(a e) -> a e", a=1).broadcast_to([P, H])).then_inc(w_const, 16)
            sp.dma_start(wr[:, :, E:NR], Wg.rearrange("(k p) n -> p k n", k=KD)).then_inc(w_const, 16)
            def norm_io(c, more=False):
                sp.wait_ge(xn_ready, c + 1)
                sp.dma_start(tab_tiles[c][:, :, 0:D], xn).then_inc(xn_stored, 16)
                sp.wait_ge(xT_cp, 2 * (c + 1))
                sp.dma_start(xT_dram[c], xnT.rearrange("p k n -> p (k n)")).then_inc(xT_stored, 16)
                if more:
                    wait_apart(sp, xn_stored, 16 * (c + 1))
                    sp.dma_start(xt, x_tiles[c + 1]).then_inc(x_loaded, 16)

            def load_xs(c):
                wait_apart(sp, xT_stored, 16 * (c + 1))
                wait_past(sp, x_split, c)
                sp.dma_start(xs[:, :, :].rearrange("p k n -> p (k n)"), xT_dram[c]).then_inc(xs_in, 16)

            def load_decay(c):
                wait_apart(sp, dec_stored, 16 * (c + 1))
                wait_past(sp, scan_done, 4 * c)
                src = decay_dram[c].rearrange("(a r) t -> a (r t)", a=1).broadcast_to([P, B * H * P])
                sp.dma_start(decay[:, :, :].rearrange("p b n -> p (b n)"), src).then_inc(dec_in, 16)

            def load_expert(e, slot):
                for m, src in enumerate((w_gate, w_up)):
                    sp.dma_start(wgu[:, slot, m].rearrange("p (k i) -> p k i", k=KD),
                                 src[e].rearrange("(k p) i -> p k i", k=KD)).then_inc(ew_in[slot], 16)
                sp.dma_start(wde[:, slot], w_down[e]).then_inc(ew_in[slot], 16)

            def load_addend(c, src):
                if not isinstance(c, int) or c > 1:
                    wait_apart(sp, wo_cp, 4 * (c - 1))
                    wait_apart(sp, res_out, 16 * (c - 1))
                sp.dma_start(addend[:, :, :], src).then_inc(add_in, 16)

            def store_res(c, dst):
                sp.wait_ge(wo_cp, 4 * c)
                sp.dma_start(dst, res[:, :, :]).then_inc(res_out, 16)

            def next_expert(c, j):
                e = (c - E0) * STEP_E + j
                sp.wait_ge(y_ps, e + 1)
                load_expert(e + 2, j % 2)

            def step(c, kind, more=True):
                first = isinstance(c, int) and c == 0
                if kind in ("norm", "lists") and not first:
                    load_addend(c, x_tiles[c - 1])
                if kind == "norm":
                    norm_io(STEP_N * c + 1, more=True)
                load_xs(c + 1)
                load_decay(c + 1)
                if kind == "norm":
                    norm_io(STEP_N * c + 2, more=True)
                    norm_io(STEP_N * c + 3, more)
                if kind == "experts":
                    for j in range(STEP_E - 1 if not isinstance(c, int) else STEP_E - 2):
                        next_expert(c, j)
                if kind in ("norm", "lists") and not first:
                    store_res(c, acc_tiles[c - 1])
                if kind == "experts":
                    wait_apart(sp, wo_cp, 4 * c)
                    sp.dma_start(aside[c - 1 - DIRECT].rearrange("p (b d) -> p b d", b=B), res[:, :, :])\
                      .then_inc(res_out, 16)
                if kind == "experts" and not isinstance(c, int):
                    next_expert(c, STEP_E - 1)

            for name, (_, src) in split_of.items():
                sp.dma_start(raw[name], src.rearrange("(k p) n -> p k n", p=P)).then_inc(w_in, 16)
            norm_io(0, more=True)
            load_xs(0)
            load_decay(0)
            step(0, "norm")
            for b in range(B):
                sp.dma_start(acc_batch[b][DIRECT * P:S, :], x_in[b][DIRECT * P:S, :]).then_inc(init_acc, 16)
            step(1, "norm")
            with sp.Fori(2, S_COUNT - 1) as c:
                step(c, "norm")
            step(S_COUNT - 1, "norm", more=False)
            step(S_COUNT, "lists")
            step(S_SLOTS, "lists")
            sp.wait_ge(idx_ready, 1)
            load_expert(0, 0)
            load_expert(1, 1)
            with sp.Fori(E0, E1 - 1) as c:
                step(c, "experts")
            step(E1 - 1, "experts")

            sp.wait_ge(scattered, 16 * NHALF * E)
            for slot in range(2):
                sp.wait_ge(gathered[slot], 16 * NHALF * (E // 2 + 1))
            load_addend(C - 1, acc_tiles[C - 2])
            sp.wait_ge(x_split, C)
            sp.dma_start(addend_end, acc_tiles[C - 1]).then_inc(add_in, 16)

            def load_old(i):
                sp.dma_start(acc_old[:, i % 2], acc_tiles[DIRECT + i]).then_inc(old_in[i % 2], 16)
                sp.dma_start(att_old[:, i % 2].rearrange("p b d -> p (b d)"), aside[i]).then_inc(old_in[i % 2], 16)

            load_old(0)
            load_old(1)
            for i in range(ASIDE):
                if i < DIRECT:
                    sp.dma_start(out_tiles[i], acc_tiles[i]).then_inc(direct_out, 16)
                sp.wait_ge(old_ready, i + 1)
                sp.dma_start(out_tiles[DIRECT + i], acc_old[:, i % 2]).then_inc(old_out, 16)
                if i + 2 < ASIDE:
                    sp.wait_ge(old_out, 16 * (i + 1))
                    load_old(i + 2)
            store_res(C - 1, out_tiles[C - 2])
            sp.wait_ge(wo_cp, 4 * C)
            sp.dma_start(out_tiles[C - 1], res_end).then_inc(res_out, 16)
            sp.wait_ge(direct_out, 16 * DIRECT)
            sp.wait_ge(old_out, 16 * ASIDE)
            sp.wait_ge(res_out, 16 * C)

        @block.gpsimd
        def _(pool):
            for m in (ident[:, :], last_row[:, :], upper[:, :], lower[:, :], before[:, :]):
                pool.memset(m, 1.0).then_inc(w_ident, 1)
            pool.memset(eye_heads[:, :, :], 1.0).then_inc(w_ident, 1)
            pool.memset(below, 1.0).then_inc(w_ident, 1)
            pool.memset(above, 1.0).then_inc(w_ident, 1)
            zeros = gated[:, 0, 0:XW]
            pool.memset(zeros, 0.0).then_inc(w_ident, 1)
            pool.wait_ge(w_ident, 9)
            pool.affine_select(out=ident[:, :], in_=ident[:, :], compare_op=ALU.is_equal, fill=0.0, base=0,
                               pattern=[[-1, P]], channel_multiplier=1).then_inc(consts, 1)
            pool.affine_select(out=last_row[:, :], in_=last_row[:, :], compare_op=ALU.is_equal, fill=0.0,
                               base=-(P - 1), pattern=[[0, P]], channel_multiplier=1).then_inc(consts, 1)
            pool.affine_select(out=upper[:, :], in_=upper[:, :], compare_op=ALU.is_ge, fill=0.0, base=0,
                               pattern=[[1, P]], channel_multiplier=-1).then_inc(consts, 1)
            pool.affine_select(out=lower[:, :], in_=lower[:, :], compare_op=ALU.is_gt, fill=0.0, base=0,
                               pattern=[[-1, P]], channel_multiplier=1).then_inc(consts, 1)
            pool.affine_select(out=before[:, :], in_=before[:, :], compare_op=ALU.is_gt, fill=0.0, base=0,
                               pattern=[[1, T]], channel_multiplier=-1).then_inc(consts, 1)
            pool.affine_select(out=eye_heads[:, :, :], in_=eye_heads[:, :, :], compare_op=ALU.is_equal, fill=0.0,
                               base=0, pattern=[[0, H], [-1, P]], channel_multiplier=1).then_inc(consts, 1)
            pool.affine_select(out=below, in_=below, compare_op=ALU.is_gt, fill=0.0, base=0,
                               pattern=[[1, G], [-1, G]], channel_multiplier=0).then_inc(consts, 1)
            pool.affine_select(out=above, in_=above, compare_op=ALU.is_gt, fill=0.0, base=0,
                               pattern=[[-1, G], [1, G]], channel_multiplier=0).then_inc(consts, 1)
            f = dict(allow_small_or_imprecise_dtypes=True)
            pool.iota(slot_col[:, :], [[P, NHALF]], base=0, channel_multiplier=1, **f).then_inc(consts, 1)
            pool.iota(trash_col[:, :], [[P, NHALF]], base=N, channel_multiplier=1, **f).then_inc(consts, 1)
            pool.memset(ones_t[:, :], 1.0).then_inc(consts, 1)
            pool.memset(sel_cur[:, :, :, 0:1], 0.0).then_inc(consts, 1)
            pool.memset(zeros_t, 0.0).then_inc(consts, 1)
            for j in range(NHALF):
                rows = slice(N + j * P, N + (j + 1) * P)
                pool.dma_start(table[rows, :], zeros).then_inc(zero_rows, 16)
                pool.dma_start(acc[rows, :], zeros[:, 0:D]).then_inc(zero_rows, 16)
            pool.wait_ge(zero_rows, 16 * 2 * NHALF)

            def decays_out(c):
                pool.wait_ge(dec_ready, c + 1)
                pool.dma_start(decay_dram[c], alphaT).then_inc(dec_stored, 16)

            def weights_out(c):
                pool.wait_ge(weight_ready, c + 1)
                pool.dma_start(tab_tiles[c][:, :, D:XW], weight).then_inc(wt_stored, 16)
                pool.tensor_copy(sel_all[:, :, :, c].rearrange("p e b -> p b e"), chosen).then_inc(sel_kept, 1)

            def gates(c):
                if not is_first(c):
                    pool.wait_ge(wo_ps, 4 * c)
                pool.wait_ge(oi_cp, at(c, 8, 8))
                for b in range(B):
                    pool.wait_ge(og_cp, 4 * c + b + 1)
                    pool.tensor_tensor(gated[:, b, :], t1[:, b, :], og[:, b, :], ALU.mult).then_inc(gate_done, 1)

            def step(c):
                if not is_first(c):
                    gates(c - 1)
                    weights_out(STEP_N * c)
                for n in range(1, STEP_N + 1):
                    decays_out(STEP_N * c + n)
                    if n < STEP_N:
                        weights_out(STEP_N * c + n)

            for name in ("og", "o"):
                w = split_of[name][0]
                pool.wait_ge(w_high, list(split_of).index(name) + 1)
                pool.tensor_tensor(w[:, 1], raw[name], w[:, 0], ALU.subtract).then_inc(w_split_pool, 1)
            decays_out(0)
            weights_out(0)
            step(0)
            step(1)
            with pool.Fori(2, S_COUNT) as c:
                step(c)
            gates(S_COUNT - 1)
            weights_out(C - 1)

            def gather(e, u):
                pool.tensor_copy(idx[:, u % 4, :], idx_all[:, e, :]).then_inc(idx_cp, 1)
                wait_apart(pool, idx_cp, e + 1)
                for j in range(NHALF):
                    pool.indirect_dma_start(
                        out=xg[:, u % 2, j, :], out_offset=None, in_=table[:, :],
                        in_offset=bass.IndirectOffsetOnAxis(ap=idx[:, u % 4, j:j + 1], axis=0),
                        bounds_check=ROWS - 1, oob_is_err=True).then_inc(gathered[u % 2], 16)

            def scatter(e, u, j):
                if not isinstance(e, int) or e + j > 0:
                    wait_apart(pool, scattered, 16 * (NHALF * e + j))
                pool.indirect_dma_start(
                    out=acc[:, :], out_offset=bass.IndirectOffsetOnAxis(ap=idx[:, u % 4, j:j + 1], axis=0),
                    in_=yb[:, u % 2, j, :], in_offset=None, bounds_check=ROWS - 1, oob_is_err=True,
                    compute_op=ALU.add).then_inc(scattered, 16)

            pool.wait_ge(cnt_cp, 1)
            pool.iota(slot_row, [[1, CAP]], base=0, channel_multiplier=0, **f).then_inc(slot_row_ready, 1)
            pool.wait_ge(slot_row_ready, 1)
            gates(S_COUNT)
            pool.wait_ge(first_cp, 1)

            def reach_group(g, u):
                wait_past(pool, tok_ps, 2 * (g - 1))
                for j in range(EB):
                    ins = pool.tensor_scalar(reach[:, u, j, :], slot_row, firsts[:, EB * g + j:EB * g + j + 1], None,
                                             ALU.is_ge)
                ins.then_inc(reach_ready, 1)

            for g in range(E // EB):
                reach_group(g, g % 2)
            pool.wait_ge(idx_ready, 1)
            pool.wait_ge(wt_stored, 16 * C)
            pool.wait_ge(xn_stored, 16 * C)
            gather(0, 0)
            gather(1, 1)
            pool.wait_ge(init_acc, 16 * B)
            def four_experts(i):
                for u in range(4):
                    e = 4 * i + u
                    pool.wait_ge(y_cp, e + 1)
                    scatter(e, u, 0)
                    gather(e + 2, u + 2)
                    scatter(e, u, 1)

            four_experts(0)
            with pool.Fori(1, E // 4) as i:
                four_experts(i)

            for i in range(ASIDE):
                pool.wait_ge(old_in[i % 2], 32 * (i // 2 + 1))
                pool.tensor_tensor(acc_old[:, i % 2], acc_old[:, i % 2], att_old[:, i % 2], ALU.add)\
                    .then_inc(old_ready, 1)

        @block.tensor
        def _(pe):
            mm, tr = pe.matmul, pe.transpose
            pe.wait_ge(consts, N_CONSTS)
            pe.wait_ge(w_const, 64)
            for k in range(KD):
                last = tr(bank[0][:, k * E:(k + 1) * E], gw_rows[:, k * P:(k + 1) * P], ident[0:E, 0:E])
            last.then_inc(gwT_ps, 1)
            pe.wait_ge(gwT_cp, 1)

            def tokens_back(c, k):
                if k == 0:
                    pe.wait_ge(xn_ready, c + 1)
                    wait_past(pe, last_cp, c)
                else:
                    pe.wait_ge(xT_cp, 2 * c + 1)
                for b in range(B):
                    last = tr(bank[7][:, b * P:(b + 1) * P], xn[:, b, k * P:(k + 1) * P], ident[:, :])
                last.then_inc(xT_ps, 1)

            def router(c):
                pe.wait_ge(xT_cp, 2 * (c + 1))
                for b in range(B):
                    for k in range(KD):
                        last = mm(bank[7][:, b * NR:(b + 1) * NR], xnT[:, k, b * P:(b + 1) * P], wr[:, k, :],
                                  start=(k == 0), stop=(k == KD - 1))
                last.then_inc(lg_ps, 1)

            def decays_across(c):
                pe.wait_ge(alpha_ready, c + 1)
                pe.wait_ge(score_ready, c + 1)
                tr(bank[7][0:B * H, 0:P], alpha.rearrange("p b h -> p (b h)"), ident[:, :]).then_inc(aT_ps, 1)

            def decays_back(c):
                wait_apart(pe, cumT_ready, c + 1)
                tr(bank[7][:, 0:B * H], cumT, ident[0:B * H, 0:B * H]).then_inc(cum_ps, 1)

            def decays_last(c):
                pe.wait_ge(cum_cp, c + 1)
                mm(bank[7][:, 0:B * H], last_row[:, :], cum_c, start=True, stop=True).then_inc(last_ps, 1)

            tokens_back(0, 0)
            tokens_back(0, 1)
            router(0)
            decays_across(0)
            decays_back(0)
            decays_last(0)

            def count_group(g):
                pe.wait_ge(selc_ready, g + 1)
                wait_past(pe, cnt_cp, g)
                if g == 0:
                    pe.wait_ge(last_cp, C)
                for j in range(EB):
                    dst = bank[7][0:T, j * P:(j + 1) * P]
                    mm(dst, sel_cur[:, g % 2, j, 1:T + 1], upper[:, :], start=True, stop=False)
                    last = mm(dst, sel_cur[:, g % 2, j, 0:T], lower[:, :], start=False, stop=True)
                last.then_inc(cnt_ps, 1)

            def first_counts():
                pe.wait_ge(cnt_cp, E // EB + 1)
                mm(bank[7][0:T, 0:E], before[:, :], totals, start=True, stop=True)
                mm(bank[7][:, E:2 * E], ones_t[:, :], totals, start=True, stop=True).then_inc(first_ps, 1)

            def slot_pair(n):
                pe.wait_ge(reach_ready, n // 2 + 1)
                wait_past(pe, tok_cnt, n)
                if n == 0:
                    pe.wait_ge(first_cp, 1)
                for j in range(2):
                    for half in range(NHALF):
                        lo = (j * NHALF + half) * P
                        last = mm(bank[7][:, lo:lo + P],
                                  reach[:, (n // 2) % 2, 2 * (n % 2) + j, half * P:(half + 1) * P],
                                  rise[:, 2 * n + j, :], start=True, stop=True)
                last.then_inc(tok_ps, 1)

            def proj_qk(c, h, which):
                u = 2 * h + which
                w = (wq, wk)[which]
                if not (isinstance(c, int) and at(c, 16, u) < 2):
                    pe.wait_ge(qk_cp, at(c, 16, u) - 1)
                for k in range(KD):
                    for i, (part, other) in enumerate(PARTS):
                        last = mm(bank[which][:, :], w[:, part, k, h * DK:(h + 1) * DK], xp[:, other, k, :],
                                  start=(k + i == 0), stop=(k == KD - 1 and i == 2))
                last.then_inc(qk_ps, 1)

            def bank4_free(c, item, b):
                first = isinstance(c, int) and c == 0
                if item == "v" and b == 0:
                    if not first:
                        pe.wait_ge(og_cp, 4 * c)
                elif item == "v":
                    pe.wait_ge(v_cp, 4 * c + b)
                elif item == "og" and b == 0:
                    pe.wait_ge(v_cp, 4 * c + 4)
                elif item == "og" and (b < 3 or first):
                    pe.wait_ge(og_cp, 4 * c + b)
                elif item == "og":
                    pe.wait_ge(wo_cp, 4 * c)
                elif b == 0:
                    pe.wait_ge(og_cp, 4 * c + 3 if not (isinstance(c, int) and c == C) else 4 * c)
                elif isinstance(c, int) and c == C:
                    pe.wait_ge(wo_cp, 4 * (c - 1) + b - 1)
                else:
                    pe.wait_ge(wo_cp, 4 * (c - 1) + b)

            def proj_tok(c, item, b):
                w, ready = {"v": (wv, v_ps), "og": (wog, og_ps)}[item]
                bank4_free(c, item, b)
                for k in range(KD):
                    for i, (part, other) in enumerate(PARTS):
                        last = mm(bank[4][:, :], xp[:, part, k, b * P:(b + 1) * P], w[:, other, k, :],
                                  start=(k + i == 0), stop=(k == KD - 1 and i == 2))
                last.then_inc(ready, 1)

            def keys_back(c, h):
                pe.wait_ge(qk_cp, at(c, 16, 2 * h + 2))
                if 5 <= h + 1 <= 8 and not (isinstance(c, int) and c == 0):
                    pe.wait_ge(ot_cp, 4 * (c - 1) + h - 3)
                elif not (isinstance(c, int) and c == 0 and h == 0):
                    pe.wait_ge(kw_cp, at(c, 8, h))
                for b in range(B):
                    last = tr(bank[3][:, b * P:(b + 1) * P], kT[:, h % 2, b * P:(b + 1) * P], ident[:, :])
                last.then_inc(kt_ps, 1)

            def scores(c, h):
                if is_last(c):
                    pe.wait_ge(qk_cp, at(c, 16, 2 * h + 2))
                if not (isinstance(c, int) and c == 0 and h == 0):
                    pe.wait_ge(a_cp, at(c, 8, h))
                for b in range(B):
                    last = mm(bank[2][:, b * P:(b + 1) * P], kT[:, h % 2, b * P:(b + 1) * P],
                              qT[:, h % 2, b * P:(b + 1) * P], start=True, stop=True)
                last.then_inc(s_ps, 1)

            def outputs(c, h):
                pe.wait_ge(a_cp, at(c, 8, h + 1))
                pe.wait_ge(v_cp, 4 * c + 4)
                if not (isinstance(c, int) and c == 0 and h == 0):
                    pe.wait_ge(oi_cp, at(c, 8, h))
                for b in range(B):
                    last = mm(bank[5][:, b * DV:(b + 1) * DV], At[:, b, :], V[:, b, h * DV:(h + 1) * DV],
                              start=True, stop=True)
                if not is_first(c):
                    pe.wait_ge(state_up, at(c - 1, 8, h + 1))
                for b in range(B if not is_first(c) else 0):
                    last = mm(bank[5][:, 256 + b * DV:256 + (b + 1) * DV], qT[:, h % 2, b * P:(b + 1) * P],
                              state[:, h, b, :], start=True, stop=True)
                last.then_inc(oi_ps, 1)

            def update(c, h):
                pe.wait_ge(kw_cp, at(c, 8, h + 1))
                if not (isinstance(c, int) and c == 0 and h == 0):
                    pe.wait_ge(state_up, at(c, 8, h))
                for b in range(B):
                    last = mm(bank[6][:, b * DV:(b + 1) * DV], kw[:, b, :], V[:, b, h * DV:(h + 1) * DV],
                              start=True, stop=True)
                last.then_inc(u_ps, 1)

            def outs_back(c, b):
                pe.wait_ge(gate_done, 4 * (c - 1) + b + 1)
                if isinstance(c, int) and c == C:
                    pe.wait_ge(ot_cp, 4 * (c - 1) + max(b - 1, 0))
                elif is_last(c):
                    pe.wait_ge(kw_cp, 8 * (C - 1))
                    pe.wait_ge(ot_cp, 4 * (c - 1) + b)
                else:
                    pe.wait_ge(kw_cp, at(c, 8, b + 4))
                for j in range(KO):
                    last = tr(back_at(c, b)[0][:, j * P:(j + 1) * P], gated[:, b, j * P:(j + 1) * P], ident[:, :])
                last.then_inc(ot_ps, 1)

            def out_proj(c, b):
                _, parts, to = back_at(c, b)
                bank4_free(c, "wo", b)
                pe.wait_ge(ot_cp, 4 * (c - 1) + b + 1)
                for j in range(KO):
                    for i, (part, other) in enumerate(PARTS):
                        last = mm(to[:, 0:D], parts[:, part, j * P:(j + 1) * P], wo[:, other, j, :],
                                  start=(j + i == 0), stop=(j == KO - 1 and i == 2))
                last.then_inc(wo_ps, 1)

            def expert_tokens(c, j):
                e = (c - E0) * STEP_E + j
                pe.wait_ge(gathered[j % 2], ((c - E0) * (STEP_E // 2) + j // 2 + 1) * 16 * NHALF)
                if j > 0:
                    pe.wait_ge(y_cp, e)
                else:
                    pe.wait_ge(scan_done, 4 * c + 1)
                for k in range(KD):
                    for half in range(NHALF):
                        lo = k * CAP + half * P
                        last = tr(bank[7][:, lo:lo + P], xg[:, j % 2, half, k * P:(k + 1) * P], ident[:, :])
                last.then_inc(xg_ps, 1)

            def expert_hidden(c, j):
                e = (c - E0) * STEP_E + j
                pe.wait_ge(wgu_split, e + 1)
                pe.wait_ge(xg_cp, e + 1)
                for m in range(2):
                    for k in range(KD):
                        for i, (part, other) in enumerate(PARTS):
                            last = mm(bank[7][:, m * CAP:(m + 1) * CAP], wgu_p[:, part, m, k * I:(k + 1) * I],
                                      xgT[:, other, k * CAP:(k + 1) * CAP], start=(k + i == 0),
                                      stop=(k == KD - 1 and i == 2))
                last.then_inc(gu_ps, 1)

            def expert_down(c, j):
                e = (c - E0) * STEP_E + j
                pe.wait_ge(h_ready, e + 1)
                for half in range(NHALF):
                    last = mm(bank[7][:, half * D:(half + 1) * D], hT[:, half * P:(half + 1) * P],
                              wde[:, j % 2, :], start=True, stop=True)
                last.then_inc(y_ps, 1)

            def beside(c, kind, s, place):
                if kind == "norm":
                    n = STEP_N * c + 1 + s // 3
                    if s % 3 == 0 and place == 1 and not (isinstance(n, int) and n == 1):
                        decays_last(n - 1)
                    if s % 3 == 1 and place in (1, 2):
                        tokens_back(n, place - 1)
                    if s % 3 == 1 and place == 3:
                        router(n)
                    if s % 3 == 2 and place == 1:
                        decays_across(n)
                    if s % 3 == 2 and place == 3:
                        decays_back(n)
                if kind == "count" and s == 0 and place == 1:
                    decays_last(C - 1)
                if kind == "count" and (s, place) in COUNT_AT:
                    count_group(COUNT_AT.index((s, place)))
                if kind == "slots" and place == 1 and s == 0:
                    first_counts()
                if kind == "slots" and s > 0:
                    slot_pair(SLOTS_S // 2 * (s - 1) + place)
                if kind == "experts" and s > 0 and place != 2:
                    {0: expert_tokens, 1: expert_hidden, 3: expert_down}[place](c, s - 1)

            def step(c, kind):
                first = isinstance(c, int) and c == 0
                pe.wait_ge(x_split, c + 1)
                proj_tok(c, "v", 0)
                proj_qk(c, 0, 0)
                beside(c, kind, 0, 1)
                proj_tok(c, "v", 1)
                proj_qk(c, 0, 1)
                proj_tok(c, "v", 2)
                if not is_last(c):
                    keys_back(c, 0)
                scores(c, 0)
                proj_tok(c, "v", 3)
                for s in range(1, H + 1):
                    if s > 1 and not is_last(c):
                        keys_back(c, s - 1)
                    if s > 1:
                        scores(c, s - 1)
                    beside(c, kind, s, 0)
                    if s in (2, 3, 8):
                        proj_tok(c, "og", min(s - 1, 3))
                    if s < H:
                        proj_qk(c, s, 0)
                    if s == 1:
                        proj_tok(c, "og", 0)
                    if s < H and kind == "experts":
                        proj_qk(c, s, 1)
                    beside(c, kind, s, 1)
                    if 4 <= s <= 7 and not first:
                        outs_back(c, s - 4)
                    if s < H and kind != "experts":
                        proj_qk(c, s, 1)
                    beside(c, kind, s, 2)
                    outputs(c, s - 1)
                    if not is_last(c):
                        update(c, s - 1)
                    if 4 <= s <= 7 and not first:
                        out_proj(c, s - 4)
                    beside(c, kind, s, 3)

            pe.wait_ge(w_split, 3)
            pe.wait_ge(w_split_pool, 2)
            step(0, "norm")
            with pe.Fori(1, S_COUNT) as c:
                step(c, "norm")
            step(S_COUNT, "count")
            step(S_SLOTS, "slots")
            with pe.Fori(E0, E1) as c:
                step(c, "experts")
            step(C - 1, "last")
            outs_back(C, 0)
            for b in range(B):
                if b + 1 < B:
                    outs_back(C, b + 1)
                out_proj(C, b)

        @block.scalar
        def _(act):
            f = nc.scalar.activation
            act.wait_ge(gwT_ps, 1)
            f(wr[:, :, 0:E], bank[0][:, 0:KD * E].rearrange("p (k e) -> p k e", k=KD), ACT.Copy).then_inc(gwT_cp, 1)

            def std_of(c):
                act.wait_ge(mv_ready, c + 1)
                f(std, mv[:, :, 1], ACT.Sqrt).then_inc(std_ready, 1)

            def sigmoids(c):
                act.wait_ge(zg_ready, c + 1)
                logits = bank[7][:, 0:B * NR].rearrange("p (b n) -> p b n", b=B)
                f(alpha, zg, ACT.Sigmoid, scale=1.0 / GATE_NORM).then_inc(alpha_ready, 1)
                wait_past(act, weight_ready, c)
                f(score, logits[:, :, 0:E], ACT.Sigmoid).then_inc(score_ready, 1)

            def tokens(c, k):
                act.wait_ge(xT_ps, 2 * c + k + 1)
                wait_past(act, xT_stored, 16 * c)
                f(xnT[:, k, :], bank[7][:, :], ACT.Copy).then_inc(xT_cp, 1)

            def tokens_high(c):
                act.wait_ge(xs_in, 16 * (c + 1))
                wait_past(act, qk_ps, 16 * c)
                wait_past(act, og_ps, 4 * c)
                f(xp[:, 0], xs[:, :, :], ACT.Copy).then_inc(x_high, 1)

            std_of(0)
            tokens(0, 0)
            tokens(0, 1)

            def weights_high(name):
                f(split_of[name][0][:, 0], raw[name], ACT.Copy).then_inc(w_high, 1)

            act.wait_ge(w_in, 16 * len(split_of))
            weights_high("v")
            weights_high("q")
            sigmoids(0)
            for name in ("k", "og", "o"):
                weights_high(name)
            tokens_high(0)

            def select_group(g):
                if g == 0:
                    act.wait_ge(sel_kept, C)
                wait_past(act, cnt_ps, g - 1)
                act.copy(sel_cur[:, g % 2, :, 1:T + 1],
                         sel_all[:, g * EB:(g + 1) * EB, :, :].rearrange("p e b c -> p e (b c)"))\
                   .then_inc(selc_ready, 1)

            def qk_copy(c, h, which):
                act.wait_ge(qk_ps, at(c, 16, 2 * h + which + 1))
                dst, scale = ((qT, 1.0), (kT, float(DK) ** -0.5))[which]
                f(dst[:, h % 2, :], bank[which][:, :], ACT.Copy, scale=scale).then_inc(qk_cp, 1)

            def v_copy(c, b):
                act.wait_ge(v_ps, 4 * c + b + 1)
                f(V[:, b, :], bank[4][:, :], ACT.Copy).then_inc(v_cp, 1)

            def og_gate(c, b):
                act.wait_ge(og_ps, 4 * c + b + 1)
                if not (isinstance(c, int) and c == 0):
                    act.wait_ge(gate_done, 4 * (c - 1) + b + 1)
                f(og[:, b, :], bank[4][:, :], ACT.Sigmoid).then_inc(og_cp, 1)

            def outs_copy(c, b):
                act.wait_ge(ot_ps, 4 * (c - 1) + b + 1)
                if isinstance(c, int) and c == C and b > 1:
                    act.wait_ge(wo_ps, 4 * (c - 1) + b - 1)
                source, parts, _ = back_at(c, b)
                f(parts[:, 0, :], source[:, :], ACT.Copy).then_inc(ot_high, 1)

            def expert_tokens(c, j):
                e = (c - E0) * STEP_E + j
                act.wait_ge(xg_ps, e + 1)
                f(xgT[:, 0, :], bank[7][:, :], ACT.Copy).then_inc(xg_high, 1)

            def weights_high_e(c, j):
                act.wait_ge(ew_in[j % 2], ((c - E0) * (STEP_E // 2) + j // 2 + 1) * 48)
                f(wgu_p[:, 0], wgu[:, j % 2], ACT.Copy).then_inc(wgu_high, 1)

            def expert_gate(c, j):
                e = (c - E0) * STEP_E + j
                act.wait_ge(gu_ps, e + 1)
                f(sg, bank[7][:, 0:CAP], ACT.Sigmoid).then_inc(sg_ready, 1)

            def beside(c, kind, s, place):
                if kind == "norm":
                    n = STEP_N * c + 1 + s // 3
                    if s % 3 == 0 and place == 1:
                        std_of(n)
                    if s % 3 == 1 and place == 1:
                        tokens(n, 0)
                    if s % 3 == 1 and place == 2:
                        tokens(n, 1)
                        sigmoids(n)
                if kind == "count" and (s, place + 1) in COUNT_AT:
                    g = COUNT_AT.index((s, place + 1))
                    if g == 0:
                        select_group(0)
                    if g + 1 < E // EB:
                        select_group(g + 1)
                if kind == "experts" and s > 0 and place < 2:
                    (expert_tokens, expert_gate)[place](c, s - 1)
                if kind == "experts" and place == 1 and 0 < s < H:
                    weights_high_e(c, s)

            def step(c, kind):
                first = isinstance(c, int) and c == 0
                v_copy(c, 0)
                qk_copy(c, 0, 0)
                if not first:
                    beside(c, kind, 0, 1)
                v_copy(c, 1)
                qk_copy(c, 0, 1)
                if first:
                    beside(c, kind, 0, 1)
                if kind == "experts":
                    weights_high_e(c, 0)
                v_copy(c, 2)
                v_copy(c, 3)
                for s in range(1, H + 1):
                    beside(c, kind, s, 0)
                    if s == H and kind != "last":
                        tokens_high(c + 1)
                    if s in (2, 3, 8):
                        og_gate(c, min(s - 1, 3))
                    if s < H:
                        qk_copy(c, s, 0)
                    if s == 1:
                        og_gate(c, 0)
                    if s < H and kind == "experts":
                        qk_copy(c, s, 1)
                    beside(c, kind, s, 1)
                    if 4 <= s <= 7 and not first:
                        outs_copy(c, s - 4)
                    if s < H and kind != "experts":
                        qk_copy(c, s, 1)
                    beside(c, kind, s, 2)

            step(0, "norm")
            with act.Fori(1, S_COUNT) as c:
                step(c, "norm")
            step(S_COUNT, "count")
            step(S_SLOTS, "slots")
            with act.Fori(E0, E1) as c:
                step(c, "experts")
            step(C - 1, "last")
            for b in range(B):
                outs_copy(C, b)

        @block.vector
        def _(dve):
            tt, ts = dve.tensor_tensor, dve.tensor_scalar

            def chained(semaphore, base):
                n = [0]

                def link(ins, apart=False):
                    n[0] += 1
                    ins.then_inc(semaphore, 1)
                    if apart:
                        wait_apart(dve, semaphore, base + n[0])
                    else:
                        dve.wait_ge(semaphore, base + n[0])
                return link, n

            dve.wait_ge(consts, N_CONSTS)
            dve.wait_ge(w_const, 64)

            def statistics(c):
                dve.wait_ge(x_loaded, 16 * (c + 1))
                link, n = chained(norm_chain, c * NORM_CHAIN)
                for b in range(B):
                    ins = dve.bn_stats(stats[:, b, :], xt[:, b, :])
                link(ins, apart=True)
                for b in range(B):
                    ins = dve.bn_aggr(mv[:, b, :], stats[:, b, :])
                link(ins)
                ts(mv[:, :, 1], mv[:, :, 1], 1e-5, None, ALU.add).then_inc(mv_ready, 1)

            def normalise(c):
                link, n = chained(norm_chain, c * NORM_CHAIN + 2)
                dve.wait_ge(std_ready, c + 1)
                link(dve.reciprocal(rstd, std))
                wait_past(dve, xn_stored, 16 * c)
                wait_past(dve, xT_ps, 2 * c)
                for b in range(B):
                    ins = ts(xn[:, b, :], xt[:, b, :], mv[:, b, 0:1], rstd[:, b:b + 1], ALU.subtract, ALU.mult)
                ins.then_inc(xn_ready, 1)

            def gates(c):
                dve.wait_ge(lg_ps, c + 1)
                logits = bank[7][:, 0:B * NR].rearrange("p (b n) -> p b n", b=B)
                tt(zg, logits[:, :, E:NR], bias_g[:, None, :].broadcast_to([P, B, H]), ALU.add).then_inc(zg_ready, 1)

            def decays_products(c):
                dve.wait_ge(aT_ps, c + 1)
                wait_past(dve, dec_stored, 16 * c)
                dve.tensor_copy(alphaT, bank[7][0:B * H, 0:P]).then_inc(aT_cp, 1)
                dve.wait_ge(aT_cp, c + 1)
                dve.tensor_tensor_scan(cumT, alphaT, zeros_t, 1.0, ALU.mult, ALU.add).then_inc(cumT_ready, 1)
                dve.wait_ge(cumT_ready, c + 1)
                dve.memset(alphaT[:, 0:1], 0.0).then_inc(dec_ready, 1)

            def decays_kept(c):
                dve.wait_ge(cum_ps, c + 1)
                dve.tensor_copy(cum_all[:, c, :, :].rearrange("p b h -> p (b h)"), bank[7][:, 0:B * H])
                dve.tensor_copy(cum_c, bank[7][:, 0:B * H]).then_inc(cum_cp, 1)

            def decays_last(c):
                dve.wait_ge(last_ps, c + 1)
                dve.tensor_copy(last_all[:, c, :, :].rearrange("p b h -> p (b h)"), bank[7][:, 0:B * H])\
                   .then_inc(last_cp, 1)

            def route_groups(c):
                link, n = chained(route_chain, c * ROUTE_CHAIN)
                dve.wait_ge(score_ready, c + 1)
                sfc_t = sfc.rearrange("p a b -> p (a b)").rearrange("p (b e) -> p b e", b=B)
                link(tt(sfc_t, score, bias_e[:, None, :].broadcast_to([P, B, E]), ALU.add))
                tt(hi1, sfc[:, :, 0:4], sfc[:, :, 4:8], ALU.max)
                link(tt(lo1, sfc[:, :, 0:4], sfc[:, :, 4:8], ALU.min))
                tt(mid, hi1[:, :, 0:2], hi1[:, :, 2:4], ALU.min)
                tt(hi2, hi1[:, :, 0:2], hi1[:, :, 2:4], ALU.max)
                link(tt(lo2, lo1[:, :, 0:2], lo1[:, :, 2:4], ALU.max))
                link(tt(lo2, lo2, mid, ALU.max))
                tt(mid[:, :, 0:1], hi2[:, :, 0:1], hi2[:, :, 1:2], ALU.min)
                tt(hi3, hi2[:, :, 0:1], hi2[:, :, 1:2], ALU.max)
                link(tt(lo3, lo2[:, :, 0:1], lo2[:, :, 1:2], ALU.max))
                link(tt(lo3, lo3, mid[:, :, 0:1], ALU.max))
                gsum = gsc.rearrange("p b g -> p (b g)")
                link(tt(gsum[:, :, None], hi3, lo3, ALU.add))
                assert n[0] == ROUTE_LINKS[0]

            def route_ranks(c):
                link, n = chained(route_chain, c * ROUTE_CHAIN + sum(ROUTE_LINKS[:1]))
                gt4 = gt.rearrange("p a b -> p (a b)").rearrange("p (b i j) -> p b i j", b=B, i=G)
                ge4 = ge.rearrange("p a b -> p (a b)").rearrange("p (b i j) -> p b i j", b=B, i=G)
                other = gsc[:, :, None, :].broadcast_to([P, B, G, G])
                own = gsc[:, :, :, None].broadcast_to([P, B, G, G])
                tt(gt4, other, own, ALU.is_gt)
                link(tt(ge4, other, own, ALU.is_ge))
                tt(gt4, gt4, above[:, None, :, :].broadcast_to([P, B, G, G]), ALU.mult)
                link(tt(ge4, ge4, below[:, None, :, :].broadcast_to([P, B, G, G]), ALU.mult))
                link(tt(gt4, gt4, ge4, ALU.add))
                link(dve.tensor_reduce(rank, gt, AX.X, ALU.add))
                link(ts(rank, rank, TG - 0.5, -BIG, ALU.is_ge, ALU.mult))
                assert n[0] == ROUTE_LINKS[1]

            def route_top(c):
                link, n = chained(route_chain, c * ROUTE_CHAIN + sum(ROUTE_LINKS[:2]))
                masked_g = masked.rearrange("p b e -> p (b e)").rearrange("p (a g) -> p a g", g=EG)
                ins = tt(masked_g, sfc, rank[:, :, None].broadcast_to([P, B * G, EG]), ALU.add)
                link(ins, apart=True)
                for b in range(B):
                    ins = dve.max(top8[:, b, :], masked[:, b, :])
                link(ins, apart=True)
                for b in range(B):
                    ins = dve.match_replace(left[:, b, :], top8[:, b, :], masked[:, b, :], -TAKEN)
                link(ins)
                assert n[0] == ROUTE_LINKS[2]

            def route_weights(c):
                link, n = chained(route_chain, c * ROUTE_CHAIN + sum(ROUTE_LINKS[:3]))
                wait_past(dve, sel_kept, c)
                wait_past(dve, wt_stored, 16 * c)
                link(tt(chosen, left, masked, ALU.not_equal))
                link(tt(weight, score, chosen, ALU.mult))
                link(dve.tensor_reduce(total, weight, AX.X, ALU.add))
                link(ts(total, total, 1e-20, None, ALU.add))
                link(dve.reciprocal(inv, total))
                dve.scalar_tensor_tensor(weight, weight, SCALE_OUT, inv[:, :, None].broadcast_to([P, B, E]),
                                         ALU.mult, ALU.mult).then_inc(weight_ready, 1)
                assert n[0] == ROUTE_LINKS[3]

            def tokens_low(c):
                dve.wait_ge(x_high, c + 1)
                tt(xp[:, 1], xs[:, :, :], xp[:, 0], ALU.subtract).then_inc(x_split, 1)

            statistics(0)
            def weights_low(name):
                w = split_of[name][0]
                dve.wait_ge(w_high, list(split_of).index(name) + 1)
                tt(w[:, 1], raw[name], w[:, 0], ALU.subtract).then_inc(w_split, 1)

            normalise(0)
            weights_low("v")
            gates(0)
            decays_products(0)
            decays_kept(0)
            decays_last(0)
            weights_low("q")
            weights_low("k")

            tab_link, _ = chained(tab_chain, 0)

            def keep_group(g):
                dve.wait_ge(cnt_ps, g + 1)
                if g == 0:
                    for left_arena in (xn_stored, xT_stored, wt_stored, dec_stored):
                        dve.wait_ge(left_arena, 16 * C)
                dve.tensor_copy(rise[:, g * EB:(g + 1) * EB, :].rearrange("p e t -> p (e t)"), bank[7][0:T, :])\
                   .then_inc(cnt_cp, 1)

            def keep_totals():
                dve.wait_ge(cnt_cp, E // EB)
                dve.tensor_copy(totals, rise[:, :, P - 1]).then_inc(cnt_cp, 1)

            def keep_firsts():
                dve.wait_ge(first_ps, 1)
                tab_link(dve.memset(rise[:, :, P - 1:P], 1.0))
                dve.tensor_copy(sums[:, :], bank[7][:, E:2 * E])
                tab_link(dve.tensor_copy(firsts, bank[7][0:T, 0:E]))
                dve.nop().then_inc(first_cp, 1)

            def count_pair(n):
                wait_past(dve, tok_cnt, n)
                dve.wait_ge(tok_ps, n + 1)
                for j in range(2 * NHALF):
                    half = j % NHALF
                    ts(junk[:, j, 0:P - 1], bank[7][:, j * P:j * P + P - 1], slot_col[:, half:half + 1], None,
                       ALU.is_le, ALU.add, accum_out=cnt[:, 2 * n + j // NHALF, half:half + 1])
                last_cols = bank[7][:, :].rearrange("p (e h t) -> p e h t", e=2, h=NHALF)[:, :, :, P - 1]
                dve.tensor_copy(tiles[:, 2 * n:2 * n + 2, :], last_cols).then_inc(tok_cnt, 1)

            def make_lists():
                dve.wait_ge(tok_cnt, E // 2)
                trash = trash_col[:, None, :].broadcast_to([P, E, NHALF])
                slots = slot_col[:, None, :].broadcast_to([P, E, NHALF])
                tab_link(dve.scalar_tensor_tensor(cnt, tiles, float(P), cnt, ALU.mult,
                                                  ALU.add))
                tab_link(dve.scalar_tensor_tensor(cnt, cnt, -float(P), trash, ALU.add,
                                                  ALU.subtract))
                tab_link(tt(tiles, sums[:, :, None].broadcast_to([P, E, NHALF]), slots, ALU.is_gt))
                tab_link(tt(cnt, cnt, tiles, ALU.mult))
                dve.tensor_copy(idx_all[:, E:E + 2, :], trash[:, 0:2, :])
                tt(idx_all[:, 0:E, :], cnt, trash, ALU.add).then_inc(idx_ready, 1)

            def decay_scans(c):
                dve.wait_ge(dec_in, 16 * (c + 1))
                for b in range(B):
                    dve.tensor_tensor_scan(Dt[:, b, :, :].rearrange("p h t -> p (h t)"), decay[:, b, :],
                                           eye_heads[:, :, :].rearrange("p h t -> p (h t)"), 0.0, ALU.mult,
                                           ALU.add).then_inc(scan_done, 1)
                dve.wait_ge(scan_done, 4 * (c + 1))

            def keys_weighted(c, h):
                dve.wait_ge(kt_ps, at(c, 8, h + 1))
                tt(kw[:, :, :], bank[3][:, :].rearrange("p (b d) -> p b d", b=B),
                   Dt[:, :, h, P - 1:P].broadcast_to([P, B, DK]), ALU.mult).then_inc(kw_cp, 1)

            def scores_decayed(c, h):
                dve.wait_ge(s_ps, at(c, 8, h + 1))
                tt(At[:, :, :], bank[2][:, :].rearrange("p (b t) -> p b t", b=B), Dt[:, :, h, :], ALU.mult)\
                    .then_inc(a_cp, 1)

            def head_out(c, h):
                part = t1[:, :, h * DV:(h + 1) * DV]
                inner = bank[5][:, 0:256].rearrange("p (b v) -> p b v", b=B)
                carried = bank[5][:, 256:512].rearrange("p (b v) -> p b v", b=B)
                added = bank[6][:, 0:256].rearrange("p (b v) -> p b v", b=B)
                if h == 0 and not is_first(c):
                    dve.wait_ge(gate_done, 4 * c)
                dve.wait_ge(oi_ps, at(c, 8, h + 1))
                if is_first(c):
                    dve.tensor_copy(part, inner).then_inc(oi_cp, 1)
                    dve.wait_ge(u_ps, at(c, 8, h + 1))
                    dve.tensor_copy(state[:, h, :, :], added).then_inc(state_up, 1)
                    return
                tt(part, carried, cum_all[:, c, :, h:h + 1].broadcast_to([P, B, DV]), ALU.mult)\
                    .then_inc(part_done, 1)
                if is_last(c):
                    dve.wait_ge(part_done, at(c - 1, 16, h + 1))
                    tt(part, part, inner, ALU.add).then_inc(oi_cp, 1)
                    return
                tt(state[:, h, :, :], state[:, h, :, :], last_all[:, c, :, h:h + 1].broadcast_to([P, B, DV]),
                   ALU.mult).then_inc(part_done, 1)
                dve.wait_ge(part_done, at(c - 1, 16, 2 * h + 1))
                tt(part, part, inner, ALU.add).then_inc(oi_cp, 1)
                dve.wait_ge(part_done, at(c - 1, 16, 2 * h + 2))
                dve.wait_ge(u_ps, at(c, 8, h + 1))
                tt(state[:, h, :, :], state[:, h, :, :], added, ALU.add).then_inc(state_up, 1)

            def gate(c, b):
                dve.wait_ge(og_cp, 4 * c + b + 1)
                dve.wait_ge(oi_cp, at(c, 8, 8))
                tt(gated[:, b, :], t1[:, b, :], og[:, b, :], ALU.mult).then_inc(gate_done, 1)

            def projected(c, b, kind):
                dve.wait_ge(wo_ps, 4 * (c - 1) + b + 1)
                if kind == "experts":
                    if b == 0:
                        dve.wait_ge(res_out, 16 * (c - 1))
                    dve.tensor_copy(res[:, b, :], bank[4][:, 0:D]).then_inc(wo_cp, 1)
                    return
                if kind == "end":
                    if b == 0:
                        dve.wait_ge(add_in, 16 * (C - ASIDE))
                    tt(res_end[:, b, :], back_at(c, b)[2][:, 0:D], addend_end[:, b, :], ALU.add).then_inc(wo_cp, 1)
                    return
                dve.wait_ge(add_in, 16 * (c if kind != "last" else C - ASIDE))
                tt(res[:, b, :], bank[4][:, 0:D], addend[:, b, :], ALU.add).then_inc(wo_cp, 1)

            def expert_hidden(c, j):
                e = (c - E0) * STEP_E + j
                dve.wait_ge(sg_ready, e + 1)
                tt(hT, bank[7][:, 0:CAP], sg, ALU.mult).then_inc(hs_ready, 1)
                dve.wait_ge(hs_ready, e + 1)
                tt(hT, hT, bank[7][:, CAP:2 * CAP], ALU.mult).then_inc(h_ready, 1)

            def outs_low(c, b):
                dve.wait_ge(ot_high, 4 * (c - 1) + b + 1)
                source, parts, _ = back_at(c, b)
                tt(parts[:, 1, :], source[:, :], parts[:, 0, :], ALU.subtract).then_inc(ot_cp, 1)

            def weights_low_e(c, j):
                dve.wait_ge(wgu_high, (c - E0) * STEP_E + j + 1)
                tt(wgu_p[:, 1], wgu[:, j % 2], wgu_p[:, 0], ALU.subtract).then_inc(wgu_split, 1)

            def tokens_low_e(c, j):
                e = (c - E0) * STEP_E + j
                dve.wait_ge(xg_high, e + 1)
                tt(xgT[:, 1, :], bank[7][:, :], xgT[:, 0, :], ALU.subtract).then_inc(xg_cp, 1)

            def expert_out(c, j):
                e = (c - E0) * STEP_E + j
                dve.wait_ge(y_ps, e + 1)
                dve.wait_ge(idx_cp, e + 2)
                for half in range(NHALF):
                    ins = ts(yb[:, j % 2, half, :], bank[7][:, half * D:(half + 1) * D],
                             xg[:, j % 2, half, bass.ds(D + e, 1)], None, ALU.mult)
                ins.then_inc(y_cp, 1)

            def beside(c, kind, s, place):
                if kind == "norm":
                    n = STEP_N * c + 1 + s // 3
                    if s % 3 == 0:
                        if place == 0 and s == 0 and is_first(c):
                            statistics(n)
                        if place == 1 and s > 0:
                            route_ranks(n - 1)
                        if place == (2 if s > 0 else 3) and not (isinstance(n, int) and n == 1):
                            decays_last(n - 1)
                        if place == (3 if s > 0 or is_first(c) else 0):
                            normalise(n)
                    if s % 3 == 1:
                        if place == 0:
                            if s == 1:
                                route_ranks(n - 1)
                            route_top(n - 1)
                        if place == 3:
                            route_weights(n - 1)
                            gates(n)
                    if s % 3 == 2 and place == 0:
                        (route_groups if s < H else decays_products)(n)
                    if s % 3 == 2 and s < H and place == 1:
                        decays_products(n)
                    if s % 3 == 2 and place == 3:
                        decays_kept(n)
                    if s % 3 == 2 and place == (2 if s < H else 3) and not (isinstance(n, int) and n == C - 1):
                        statistics(n + 1)
                    if s == H and place == 3:
                        route_groups(n)
                if kind == "count" and s == 0 and place == 3:
                    for part in (decays_last, route_ranks, route_top, route_weights):
                        part(C - 1)
                if kind == "count" and s > 0:
                    for pe_place in {2: (1, 2), 3: (3,)}.get(place, ()):
                        if (s, pe_place) in COUNT_AT:
                            keep_group(COUNT_AT.index((s, pe_place)))
                    if place == 3 and s == H:
                        keep_totals()
                if kind == "slots" and s == 0 and place == 3:
                    keep_firsts()
                if kind == "slots" and s > 0:
                    n = SLOTS_S // 2 * (s - 1) + place
                    count_pair(n)
                    if n == E // 2 - 1:
                        make_lists()
                if kind == "experts" and s == 0 and place == 3:
                    weights_low_e(c, 0)
                if kind == "experts" and s > 0:
                    if place == 0:
                        tokens_low_e(c, s - 1)
                    if place == 2:
                        expert_hidden(c, s - 1)
                        if s < H:
                            weights_low_e(c, s)
                    if place == 3:
                        expert_out(c, s - 1)

            def step(c, kind):
                beside(c, kind, 0, 0)
                beside(c, kind, 0, 1)
                decay_scans(c)
                beside(c, kind, 0, 3)
                for s in range(1, H + 1):
                    if not is_last(c):
                        keys_weighted(c, s - 1)
                    scores_decayed(c, s - 1)
                    if s == 1 and kind in ("experts", "last"):
                        for b in range(B):
                            gate(c - 1, b)
                    early = kind in ("slots", "experts") or (kind == "norm" and s == 6)
                    if early:
                        beside(c, kind, s, 0)
                    if 4 <= s <= 7 and not is_first(c):
                        outs_low(c, s - 4)
                    if not early:
                        beside(c, kind, s, 0)
                    beside(c, kind, s, 1)
                    beside(c, kind, s, 2)
                    if s == H and kind != "last":
                        tokens_low(c + 1)
                    head_out(c, s - 1)
                    if kind == "norm":
                        beside(c, kind, s, 3)
                    if 4 <= s <= 7 and not is_first(c):
                        projected(c, s - 4, kind)
                    if kind != "norm":
                        beside(c, kind, s, 3)

            tokens_low(0)
            route_groups(0)
            step(0, "norm")
            with dve.Fori(1, S_COUNT - 1) as c:
                step(c, "norm")
            step(S_COUNT - 1, "norm")
            step(S_COUNT, "count")
            step(S_SLOTS, "slots")
            with dve.Fori(E0, E1) as c:
                step(c, "experts")
            step(C - 1, "last")
            for b in range(B):
                gate(C - 1, b)
            outs_low(C, 0)
            outs_low(C, 1)
            for b in range(B):
                projected(C, b, "end")
                if b + 2 < B:
                    outs_low(C, b + 2)


_INS = ["L0_attn_x", "L0_attn_Wq", "L0_attn_Wk", "L0_attn_Wv", "L0_attn_Wo", "L0_attn_Wg", "L0_attn_bg",
        "L0_attn_Wog", "L0_ffn_gate_w", "L0_ffn_gate_bias", "L0_ffn_w_gate", "L0_ffn_w_up", "L0_ffn_w_down"]
_OUTS = [((4, 2048, 256), "float32")]


def kernel(**inputs):
    import numpy as _np
    import concourse.bacc as _bacc
    from concourse import mybir as _mybir
    from concourse.bass_utils import run_bass_kernel_spmd as _run

    nc = _bacc.Bacc("TRN2", target_bir_lowering=False, num_devices=1)
    arrays, args = {}, []
    for name in _INS:
        a = _np.ascontiguousarray(inputs[name])
        arrays[f"in_{name}_dram"] = a
        args.append(nc.dram_tensor(f"in_{name}_dram", a.shape, _mybir.dt.from_np(a.dtype), kind="ExternalInput").ap())
    for i, (shape, dtype) in enumerate(_OUTS):
        dt = _mybir.dt.from_np(_np.dtype(dtype))
        args.append(nc.dram_tensor(f"out_{i}_dram", shape, dt, kind="ExternalOutput").ap())
    build(nc, *args)
    r = _run(nc, [arrays], core_ids=[0])
    return r.results[0]["out_0_dram"]
```
